# Optimizing a Trainium2 kernel written in Bass

```python
import numpy as np
import jax
import jax.numpy as jnp

def _softmax(x, axis=-1):
    return jax.nn.softmax(x, axis=axis)

def _gelu(x):
    return jax.nn.gelu(x, approximate=True)

def _silu(x):
    return jax.nn.silu(x)

def _sigmoid(x):
    return jax.nn.sigmoid(x)

def _layernorm(x, axis=-1, eps=1e-05):
    m = jnp.mean(x, axis=axis, keepdims=True)
    v = jnp.var(x, axis=axis, keepdims=True)
    return (x - m) / jnp.sqrt(v + eps)

def _scatter_add(tgt, idx, src, axis=0):
    return tgt.at[idx].add(src)

def _segment_sum(src, seg, n):
    return jax.ops.segment_sum(src, seg, n)
kernel_name = 'mk_seq_preln_d2_jaxref_r8_dab80b'

def setup_inputs(seed: int=0):
    np.random.seed(seed)
    _w = jnp.asarray

    def _L0_attn_setup():
        import jax, jax.numpy as jnp
        import numpy as np
        N_HEAD = 16
        D_MODEL = 128
        HEAD_DIM = D_MODEL // N_HEAD
        LAMBDA_INIT = 0.8 - 0.6 * float(np.exp(-0.3 * 1))

        def _rms_norm(x):
            eps = jnp.finfo(x.dtype).eps
            return x * jax.lax.rsqrt(jnp.mean(jnp.square(x), axis=-1, keepdims=True) + eps)

        def _rotary_cos_sin(T, dim, base=10000.0):
            inv_freq = 1.0 / base ** (jnp.arange(0, dim, 2, dtype=jnp.float32) / dim)
            freqs = jnp.outer(jnp.arange(T, dtype=jnp.float32), inv_freq)
            return (jnp.cos(freqs), jnp.sin(freqs))

        def _apply_rotary(x, cos, sin):
            d = x.shape[-1] // 2
            c = cos[None, :, None, None, :]
            s = sin[None, :, None, None, :]
            x1, x2 = (x[..., :d], x[..., d:])
            return jnp.concatenate([x1 * c + x2 * s, -x1 * s + x2 * c], axis=-1)

        def _causal_attn(q, k, v, scale):
            T = q.shape[1]
            scores = jnp.einsum('bthd,bshd->bhts', q, k) * scale
            mask = jnp.tril(jnp.ones((T, T), dtype=bool))
            scores = jnp.where(mask, scores, -jnp.inf)
            w = jax.nn.softmax(scores, axis=-1)
            return jnp.einsum('bhts,bshd->bthd', w, v)
        key = jax.random.key(seed)
        ks = jax.random.split(key, 10)
        B, T, D = (1, 256, D_MODEL)
        std = 0.02
        return {'x': jax.random.normal(ks[0], (B, T, D), jnp.float32), 'Wq': jax.random.normal(ks[1], (D, D), jnp.float32) * std, 'Wk': jax.random.normal(ks[2], (D, D), jnp.float32) * std, 'Wv': jax.random.normal(ks[3], (D, D), jnp.float32) * std, 'Wproj': jax.random.normal(ks[4], (D, D), jnp.float32) * std, 'lambda_q1': jax.random.normal(ks[5], (HEAD_DIM // 2,), jnp.float32) * 0.1, 'lambda_k1': jax.random.normal(ks[6], (HEAD_DIM // 2,), jnp.float32) * 0.1, 'lambda_q2': jax.random.normal(ks[7], (HEAD_DIM // 2,), jnp.float32) * 0.1, 'lambda_k2': jax.random.normal(ks[8], (HEAD_DIM // 2,), jnp.float32) * 0.1}
    _L0_attn_in = _L0_attn_setup()

    def _L0_ffn_setup():
        import jax, jax.numpy as jnp
        import numpy as np
        B, S, D = (2, 256, 128)
        H, HKV = (16, 4)
        HD = D // H
        F, E, K = (256, 8, 2)
        THETA = 10000.0
        EPS = 1e-05

        def _rmsnorm(x, w):
            return x * jax.lax.rsqrt(jnp.mean(x * x, axis=-1, keepdims=True) + EPS) * w

        def _rope_cos_sin(seq_len, head_dim, theta):
            inv_freq = 1.0 / theta ** (jnp.arange(0, head_dim, 2, dtype=jnp.float32) / head_dim)
            freqs = jnp.arange(seq_len, dtype=jnp.float32)[:, None] * inv_freq
            return (jnp.cos(freqs), jnp.sin(freqs))

        def _apply_rope(x, cos, sin):
            x1, x2 = jnp.split(x, 2, axis=-1)
            c = cos[None, :, None, :]
            s = sin[None, :, None, :]
            return jnp.concatenate([x1 * c - x2 * s, x2 * c + x1 * s], axis=-1)
        key = jax.random.key(seed)
        ks = jax.random.split(key, 12)
        s = 0.02
        return {'hidden_states': jax.random.normal(ks[0], (B, S, D), jnp.float32), 'ln1_w': 1.0 + 0.1 * jax.random.normal(ks[1], (D,), jnp.float32), 'ln2_w': 1.0 + 0.1 * jax.random.normal(ks[2], (D,), jnp.float32), 'Wq': s * jax.random.normal(ks[3], (D, H * HD), jnp.float32), 'Wk': s * jax.random.normal(ks[4], (D, HKV * HD), jnp.float32), 'Wv': s * jax.random.normal(ks[5], (D, HKV * HD), jnp.float32), 'Wo': s * jax.random.normal(ks[6], (H * HD, D), jnp.float32), 'Wr': s * jax.random.normal(ks[7], (D, E), jnp.float32), 'Wg': s * jax.random.normal(ks[8], (E, D, F), jnp.float32), 'Wu': s * jax.random.normal(ks[9], (E, D, F), jnp.float32), 'Wd': s * jax.random.normal(ks[10], (E, F, D), jnp.float32)}
    _L0_ffn_in = _L0_ffn_setup()

    def _L1_attn_setup():
        import jax, jax.numpy as jnp
        import numpy as np
        NUM_BLOCKS = 8
        D = 128
        FF = 512
        B, S = (4, 512)
        EPS_ATTN = 1e-06
        EPS_LN = 1e-06

        def _ln(x, scale, bias):
            m = jnp.mean(x, axis=-1, keepdims=True)
            v = jnp.var(x, axis=-1, keepdims=True)
            return (x - m) * jax.lax.rsqrt(v + EPS_LN) * scale + bias

        def _forward(x, Wq, bq, Wk, bk, Wv, bv, Wo, bo, ln1_s, ln1_b, W1, b1, W2, b2, ln2_s, ln2_b):
            gelu = lambda t: jax.nn.gelu(t, approximate=True)
            fmap = lambda t: jax.nn.elu(t) + 1.0
            for i in range(NUM_BLOCKS):
                residual = x
                Q = fmap(x @ Wq[i] + bq[i])
                K = fmap(x @ Wk[i] + bk[i])
                value = x @ Wv[i] + bv[i]
                KV = jnp.einsum('nsh,nsh->nh', K, value)
                Ksum = jnp.sum(K, axis=1)
                Z = 1.0 / (Q * Ksum[:, None, :] + EPS_ATTN)
                V = Q * KV[:, None, :] * Z
                attn_out = gelu(V @ Wo[i] + bo[i])
                x = _ln(attn_out + residual, ln1_s[i], ln1_b[i])
                residual = x
                h = gelu(x @ W1[i] + b1[i])
                ff_out = gelu(h @ W2[i] + b2[i])
                x = _ln(ff_out + residual, ln2_s[i], ln2_b[i])
            return x
        key = jax.random.key(seed)
        ks = jax.random.split(key, 16)
        g = lambda k, shape, fan: jax.random.normal(k, shape, jnp.float32) * (1.0 / np.sqrt(fan))
        inp = {'x': jax.random.normal(ks[0], (B, S, D), jnp.float32), 'Wq': g(ks[1], (NUM_BLOCKS, D, D), D), 'bq': jnp.zeros((NUM_BLOCKS, D), jnp.float32), 'Wk': g(ks[2], (NUM_BLOCKS, D, D), D), 'bk': jnp.zeros((NUM_BLOCKS, D), jnp.float32), 'Wv': g(ks[3], (NUM_BLOCKS, D, D), D), 'bv': jnp.zeros((NUM_BLOCKS, D), jnp.float32), 'Wo': g(ks[4], (NUM_BLOCKS, D, D), D), 'bo': jnp.zeros((NUM_BLOCKS, D), jnp.float32), 'ln1_s': jnp.ones((NUM_BLOCKS, D), jnp.float32), 'ln1_b': jnp.zeros((NUM_BLOCKS, D), jnp.float32), 'W1': g(ks[5], (NUM_BLOCKS, D, FF), D), 'b1': jnp.zeros((NUM_BLOCKS, FF), jnp.float32), 'W2': g(ks[6], (NUM_BLOCKS, FF, D), FF), 'b2': jnp.zeros((NUM_BLOCKS, D), jnp.float32), 'ln2_s': jnp.ones((NUM_BLOCKS, D), jnp.float32), 'ln2_b': jnp.zeros((NUM_BLOCKS, D), jnp.float32)}
        return inp
    _L1_attn_in = _L1_attn_setup()

    def _L1_ffn_setup():
        import jax, jax.numpy as jnp
        import numpy as np

        def _bitlinear(x, w_latent):
            scale = jax.lax.stop_gradient(jnp.clip(jnp.mean(jnp.abs(w_latent), axis=1, keepdims=True), 1e-05, None))
            tern = jnp.clip(jnp.round(w_latent / scale), -1.0, 1.0)
            w = w_latent + jax.lax.stop_gradient(tern - w_latent)
            return x @ (w * scale).T
        key = jax.random.key(seed)
        ks = jax.random.split(key, 6)
        dim, hidden, rank = (128, 512, 16)
        B, S = (4, 512)
        x = jax.random.normal(ks[0], (B, S, dim), dtype=jnp.float32)
        w_fc = 0.02 * jax.random.normal(ks[1], (hidden, dim), dtype=jnp.float32)
        w_proj = 0.02 * jax.random.normal(ks[2], (dim, hidden), dtype=jnp.float32)
        u = 0.02 * jax.random.normal(ks[3], (hidden, rank), dtype=jnp.float32)
        v = 0.02 * jax.random.normal(ks[4], (rank, dim), dtype=jnp.float32)
        fast_b = jax.random.normal(ks[5], (rank, rank), dtype=jnp.float32)
        gate = jnp.float32(0.05)
        return {'x': x, 'fast_b': fast_b, 'w_fc': w_fc, 'w_proj': w_proj, 'u': u, 'v': v, 'gate': gate}
    _L1_ffn_in = _L1_ffn_setup()
    _d = {'L0_attn_x': _L0_attn_in['x'], 'L0_attn_Wq': _L0_attn_in['Wq'], 'L0_attn_Wk': _L0_attn_in['Wk'], 'L0_attn_Wv': _L0_attn_in['Wv'], 'L0_attn_Wproj': _L0_attn_in['Wproj'], 'L0_attn_lambda_q1': _L0_attn_in['lambda_q1'], 'L0_attn_lambda_k1': _L0_attn_in['lambda_k1'], 'L0_attn_lambda_q2': _L0_attn_in['lambda_q2'], 'L0_attn_lambda_k2': _L0_attn_in['lambda_k2'], 'L0_ffn_ln1_w': _L0_ffn_in['ln1_w'], 'L0_ffn_ln2_w': _L0_ffn_in['ln2_w'], 'L0_ffn_Wq': _L0_ffn_in['Wq'], 'L0_ffn_Wk': _L0_ffn_in['Wk'], 'L0_ffn_Wv': _L0_ffn_in['Wv'], 'L0_ffn_Wo': _L0_ffn_in['Wo'], 'L0_ffn_Wr': _L0_ffn_in['Wr'], 'L0_ffn_Wg': _L0_ffn_in['Wg'], 'L0_ffn_Wu': _L0_ffn_in['Wu'], 'L0_ffn_Wd': _L0_ffn_in['Wd'], 'L1_attn_Wq': _L1_attn_in['Wq'], 'L1_attn_bq': _L1_attn_in['bq'], 'L1_attn_Wk': _L1_attn_in['Wk'], 'L1_attn_bk': _L1_attn_in['bk'], 'L1_attn_Wv': _L1_attn_in['Wv'], 'L1_attn_bv': _L1_attn_in['bv'], 'L1_attn_Wo': _L1_attn_in['Wo'], 'L1_attn_bo': _L1_attn_in['bo'], 'L1_attn_ln1_s': _L1_attn_in['ln1_s'], 'L1_attn_ln1_b': _L1_attn_in['ln1_b'], 'L1_attn_W1': _L1_attn_in['W1'], 'L1_attn_b1': _L1_attn_in['b1'], 'L1_attn_W2': _L1_attn_in['W2'], 'L1_attn_b2': _L1_attn_in['b2'], 'L1_attn_ln2_s': _L1_attn_in['ln2_s'], 'L1_attn_ln2_b': _L1_attn_in['ln2_b'], 'L1_ffn_fast_b': _L1_ffn_in['fast_b'], 'L1_ffn_w_fc': _L1_ffn_in['w_fc'], 'L1_ffn_w_proj': _L1_ffn_in['w_proj'], 'L1_ffn_u': _L1_ffn_in['u'], 'L1_ffn_v': _L1_ffn_in['v'], 'L1_ffn_gate': _L1_ffn_in['gate']}
    _x0 = _d['L0_attn_x']
    _d['L0_attn_x'] = jax.random.normal(jax.random.fold_in(jax.random.key(seed), 1), (16, 512, 128), dtype=_x0.dtype)
    del _x0
    return _d

def reference(L0_attn_x, L0_attn_Wq, L0_attn_Wk, L0_attn_Wv, L0_attn_Wproj, L0_attn_lambda_q1, L0_attn_lambda_k1, L0_attn_lambda_q2, L0_attn_lambda_k2, L0_ffn_ln1_w, L0_ffn_ln2_w, L0_ffn_Wq, L0_ffn_Wk, L0_ffn_Wv, L0_ffn_Wo, L0_ffn_Wr, L0_ffn_Wg, L0_ffn_Wu, L0_ffn_Wd, L1_attn_Wq, L1_attn_bq, L1_attn_Wk, L1_attn_bk, L1_attn_Wv, L1_attn_bv, L1_attn_Wo, L1_attn_bo, L1_attn_ln1_s, L1_attn_ln1_b, L1_attn_W1, L1_attn_b1, L1_attn_W2, L1_attn_b2, L1_attn_ln2_s, L1_attn_ln2_b, L1_ffn_fast_b, L1_ffn_w_fc, L1_ffn_w_proj, L1_ffn_u, L1_ffn_v, L1_ffn_gate):

    def _L0_attn_ref(x, Wq, Wk, Wv, Wproj, lambda_q1, lambda_k1, lambda_q2, lambda_k2):
        import jax, jax.numpy as jnp
        import numpy as np
        N_HEAD = 16
        D_MODEL = 128
        HEAD_DIM = D_MODEL // N_HEAD
        LAMBDA_INIT = 0.8 - 0.6 * float(np.exp(-0.3 * 1))

        def _rms_norm(x):
            eps = jnp.finfo(x.dtype).eps
            return x * jax.lax.rsqrt(jnp.mean(jnp.square(x), axis=-1, keepdims=True) + eps)

        def _rotary_cos_sin(T, dim, base=10000.0):
            inv_freq = 1.0 / base ** (jnp.arange(0, dim, 2, dtype=jnp.float32) / dim)
            freqs = jnp.outer(jnp.arange(T, dtype=jnp.float32), inv_freq)
            return (jnp.cos(freqs), jnp.sin(freqs))

        def _apply_rotary(x, cos, sin):
            d = x.shape[-1] // 2
            c = cos[None, :, None, None, :]
            s = sin[None, :, None, None, :]
            x1, x2 = (x[..., :d], x[..., d:])
            return jnp.concatenate([x1 * c + x2 * s, -x1 * s + x2 * c], axis=-1)

        def _causal_attn(q, k, v, scale):
            T = q.shape[1]
            scores = jnp.einsum('bthd,bshd->bhts', q, k) * scale
            mask = jnp.tril(jnp.ones((T, T), dtype=bool))
            scores = jnp.where(mask, scores, -jnp.inf)
            w = jax.nn.softmax(scores, axis=-1)
            return jnp.einsum('bhts,bshd->bthd', w, v)
        B, T, D = x.shape
        nh, hd = (N_HEAD, HEAD_DIM)
        q = (x @ Wq.T).reshape(B, T, 2, nh // 2, hd)
        k = (x @ Wk.T).reshape(B, T, 2, nh // 2, hd)
        v = (x @ Wv.T).reshape(B, T, nh // 2, 2 * hd)
        q, k = (_rms_norm(q), _rms_norm(k))
        cos, sin = _rotary_cos_sin(T, hd)
        q, k = (_apply_rotary(q, cos, sin), _apply_rotary(k, cos, sin))
        q1, q2 = (q[:, :, 0], q[:, :, 1])
        k1, k2 = (k[:, :, 0], k[:, :, 1])
        scale = 1.0 / jnp.sqrt(jnp.asarray(hd, x.dtype))
        y1 = _causal_attn(q1, k1, v, scale)
        y2 = _causal_attn(q2, k2, v, scale)
        lambda_1 = jnp.exp(jnp.sum(lambda_q1 * lambda_k1))
        lambda_2 = jnp.exp(jnp.sum(lambda_q2 * lambda_k2))
        lambda_full = lambda_1 - lambda_2 + LAMBDA_INIT
        y = (y1 - lambda_full * y2).reshape(B, T, D)
        return y @ Wproj.T

    def _L0_ffn_ref(hidden_states, ln1_w, ln2_w, Wq, Wk, Wv, Wo, Wr, Wg, Wu, Wd):
        import jax, jax.numpy as jnp
        import numpy as np
        B, S, D = (2, 256, 128)
        H, HKV = (16, 4)
        HD = D // H
        F, E, K = (256, 8, 2)
        THETA = 10000.0
        EPS = 1e-05

        def _rmsnorm(x, w):
            return x * jax.lax.rsqrt(jnp.mean(x * x, axis=-1, keepdims=True) + EPS) * w

        def _rope_cos_sin(seq_len, head_dim, theta):
            inv_freq = 1.0 / theta ** (jnp.arange(0, head_dim, 2, dtype=jnp.float32) / head_dim)
            freqs = jnp.arange(seq_len, dtype=jnp.float32)[:, None] * inv_freq
            return (jnp.cos(freqs), jnp.sin(freqs))

        def _apply_rope(x, cos, sin):
            x1, x2 = jnp.split(x, 2, axis=-1)
            c = cos[None, :, None, :]
            s = sin[None, :, None, :]
            return jnp.concatenate([x1 * c - x2 * s, x2 * c + x1 * s], axis=-1)
        b, s, d = hidden_states.shape
        residual = hidden_states
        h = _rmsnorm(hidden_states, ln1_w)
        q = (h @ Wq).reshape(b, s, H, HD)
        k = (h @ Wk).reshape(b, s, HKV, HD)
        v = (h @ Wv).reshape(b, s, HKV, HD)
        cos, sin = _rope_cos_sin(s, HD, THETA)
        q = _apply_rope(q, cos, sin)
        k = _apply_rope(k, cos, sin)
        rep = H // HKV
        k = jnp.repeat(k, rep, axis=2)
        v = jnp.repeat(v, rep, axis=2)
        scores = jnp.einsum('bqhd,bkhd->bhqk', q, k) / np.sqrt(HD).astype(np.float32)
        causal = jnp.tril(jnp.ones((s, s), dtype=bool))
        scores = jnp.where(causal[None, None], scores, jnp.finfo(scores.dtype).min)
        attn = jax.nn.softmax(scores, axis=-1)
        ctx = jnp.einsum('bhqk,bkhd->bqhd', attn, v).reshape(b, s, H * HD)
        attn_out = ctx @ Wo
        h = jnp.clip(residual + attn_out, -100.0, 100.0)
        residual = h
        hn = _rmsnorm(h, ln2_w)
        flat = hn.reshape(b * s, d)
        logits = flat @ Wr
        probs = jax.nn.softmax(logits, axis=-1)
        topv, topi = jax.lax.top_k(probs, K)
        topv = topv / jnp.sum(topv, axis=-1, keepdims=True)
        w = jnp.sum(jax.nn.one_hot(topi, E, dtype=flat.dtype) * topv[..., None], axis=1)
        g = jnp.einsum('td,edf->etf', flat, Wg)
        u = jnp.einsum('td,edf->etf', flat, Wu)
        a = jax.nn.silu(g) * u
        o = jnp.einsum('etf,efd->etd', a, Wd)
        moe_out = jnp.einsum('te,etd->td', w, o).reshape(b, s, d)
        out = jnp.clip(residual + moe_out, -100.0, 100.0)
        return out

    def _L1_attn_ref(x, Wq, bq, Wk, bk, Wv, bv, Wo, bo, ln1_s, ln1_b, W1, b1, W2, b2, ln2_s, ln2_b):
        import jax, jax.numpy as jnp
        import numpy as np
        NUM_BLOCKS = 8
        D = 128
        FF = 512
        B, S = (4, 512)
        EPS_ATTN = 1e-06
        EPS_LN = 1e-06

        def _ln(x, scale, bias):
            m = jnp.mean(x, axis=-1, keepdims=True)
            v = jnp.var(x, axis=-1, keepdims=True)
            return (x - m) * jax.lax.rsqrt(v + EPS_LN) * scale + bias

        def _forward(x, Wq, bq, Wk, bk, Wv, bv, Wo, bo, ln1_s, ln1_b, W1, b1, W2, b2, ln2_s, ln2_b):
            gelu = lambda t: jax.nn.gelu(t, approximate=True)
            fmap = lambda t: jax.nn.elu(t) + 1.0
            for i in range(NUM_BLOCKS):
                residual = x
                Q = fmap(x @ Wq[i] + bq[i])
                K = fmap(x @ Wk[i] + bk[i])
                value = x @ Wv[i] + bv[i]
                KV = jnp.einsum('nsh,nsh->nh', K, value)
                Ksum = jnp.sum(K, axis=1)
                Z = 1.0 / (Q * Ksum[:, None, :] + EPS_ATTN)
                V = Q * KV[:, None, :] * Z
                attn_out = gelu(V @ Wo[i] + bo[i])
                x = _ln(attn_out + residual, ln1_s[i], ln1_b[i])
                residual = x
                h = gelu(x @ W1[i] + b1[i])
                ff_out = gelu(h @ W2[i] + b2[i])
                x = _ln(ff_out + residual, ln2_s[i], ln2_b[i])
            return x
        return _forward(x, Wq, bq, Wk, bk, Wv, bv, Wo, bo, ln1_s, ln1_b, W1, b1, W2, b2, ln2_s, ln2_b)

    def _L1_ffn_ref(x, fast_b, w_fc, w_proj, u, v, gate):
        import jax, jax.numpy as jnp
        import numpy as np

        def _bitlinear(x, w_latent):
            scale = jax.lax.stop_gradient(jnp.clip(jnp.mean(jnp.abs(w_latent), axis=1, keepdims=True), 1e-05, None))
            tern = jnp.clip(jnp.round(w_latent / scale), -1.0, 1.0)
            w = w_latent + jax.lax.stop_gradient(tern - w_latent)
            return x @ (w * scale).T
        h = _bitlinear(x, w_fc) + gate * (x @ v.T @ fast_b.T @ u.T)
        r = jnp.maximum(h, 0.0)
        return _bitlinear(r * r, w_proj)
    x = L0_attn_x
    x = x + _L0_attn_ref(_layernorm(x, axis=-1), L0_attn_Wq, L0_attn_Wk, L0_attn_Wv, L0_attn_Wproj, L0_attn_lambda_q1, L0_attn_lambda_k1, L0_attn_lambda_q2, L0_attn_lambda_k2)
    x = x + _L0_ffn_ref(_layernorm(x, axis=-1), L0_ffn_ln1_w, L0_ffn_ln2_w, L0_ffn_Wq, L0_ffn_Wk, L0_ffn_Wv, L0_ffn_Wo, L0_ffn_Wr, L0_ffn_Wg, L0_ffn_Wu, L0_ffn_Wd)
    x = x + _L1_attn_ref(_layernorm(x, axis=-1), L1_attn_Wq, L1_attn_bq, L1_attn_Wk, L1_attn_bk, L1_attn_Wv, L1_attn_bv, L1_attn_Wo, L1_attn_bo, L1_attn_ln1_s, L1_attn_ln1_b, L1_attn_W1, L1_attn_b1, L1_attn_W2, L1_attn_b2, L1_attn_ln2_s, L1_attn_ln2_b)
    x = x + _L1_ffn_ref(_layernorm(x, axis=-1), L1_ffn_fast_b, L1_ffn_w_fc, L1_ffn_w_proj, L1_ffn_u, L1_ffn_v, L1_ffn_gate)
    return x

_drawn_inputs = setup_inputs


def setup_inputs(seed=0):
    import zlib

    import numpy as np

    out = dict(_drawn_inputs(seed))
    spreads = {'L1_attn_bq': (0.0, 0.8),
     'L1_attn_bk': (0.0, 0.8),
     'L1_attn_bv': (0.0, 0.1),
     'L1_attn_bo': (0.0, 0.1),
     'L1_attn_ln1_s': (1.0, 0.2),
     'L1_attn_ln1_b': (0.0, 0.1),
     'L1_attn_b1': (0.0, 0.1),
     'L1_attn_b2': (0.0, 0.1),
     'L1_attn_ln2_s': (1.0, 0.2),
     'L1_attn_ln2_b': (0.0, 0.1)}
    factors = {'L0_attn_Wq': 8.0,
     'L0_attn_Wk': 8.0,
     'L0_attn_Wv': 7.847,
     'L0_attn_Wproj': 7.86,
     'L0_attn_lambda_q1': 8.0,
     'L0_attn_lambda_k1': 8.0,
     'L0_attn_lambda_q2': 8.0,
     'L0_attn_lambda_k2': 8.0,
     'L0_ffn_ln1_w': 8.0,
     'L0_ffn_ln2_w': 8.0,
     'L0_ffn_Wq': 8.0,
     'L0_ffn_Wk': 8.0,
     'L0_ffn_Wv': 8.0,
     'L0_ffn_Wo': 8.0,
     'L0_ffn_Wr': 8.0,
     'L0_ffn_Wg': 8.0,
     'L0_ffn_Wu': 8.0,
     'L0_ffn_Wd': 8.0,
     'L1_attn_Wq': 8.0,
     'L1_ffn_fast_b': 8.0,
     'L1_ffn_w_fc': 8.0,
     'L1_ffn_w_proj': 8.0,
     'L1_ffn_u': 8.0,
     'L1_ffn_v': 8.0}
    for name, (base, spread) in spreads.items():
        noise = np.random.default_rng([zlib.crc32(name.encode()), seed]).standard_normal(out[name].shape)
        drawn = base * np.exp(spread * noise) if base else spread * noise
        out[name] = jnp.asarray(drawn.astype(out[name].dtype))
    for name, factor in factors.items():
        out[name] = (out[name] * factor).astype(out[name].dtype)
    return out
```

```python
from contextlib import ExitStack

import concourse.bass as bass
from concourse import mybir

F32 = mybir.dt.float32
BF16 = mybir.dt.bfloat16
ALU = mybir.AluOpType
ACT = mybir.ActivationFunctionType
AX = mybir.AxisListType
P = 128
SEQ = 512
NT = SEQ // P
HD = 8
NH = 16
SLOT = 64
SPLIT = 6
BIG = -1.0e30
SCALE = float(HD) ** -0.5
LN_EPS = 1e-5
OFF_DIAG = {0: (512, 384), 2: (896, 128), 1: (1024, 256)}
HEAD_COLS = 1280


def ds(start, size):
    return bass.ds(start, size)


def tile_of(T, b, t):
    return T[:, ds(NT * b + t, 1), :].rearrange("p a d -> p (a d)")


def attention_stage(nc, C, XT, OUT, A, gqa, NB):
    VD = 8 if gqa else 16
    NV = 4 if gqa else 8
    NK = 4 if gqa else 16
    QK = P + (32 if gqa else P)
    QKV = QK + (32 if gqa else P)
    KP = 4 if gqa else 8
    KROWS = 51 if gqa else 48
    NHK = QK // HD

    def head(s):
        g, c = s // 4, s % 4
        if gqa:
            return s // 2, g, 64 * (s % 2), g
        h = 2 * g + (c % 2) + 8 * (c // 2)
        return h // 2, h // 2, 64 * (h % 2), 2 * g + c % 2

    with ExitStack() as ctx:
        def sb(name, shape, dt=F32):
            return ctx.enter_context(nc.sbuf_tensor(A + name, shape, dt))

        def sem(name):
            return C["sems"].enter_context(nc.semaphore(A + name))

        wqkv = sb("wqkv", [P, QKV])
        wout = sb("wout", [P, P])
        lnw = sb("lnw", [P, 2])
        lam = sb("lam", [P, 4, 4])
        lam_s = sb("lam_s", [P, 8])
        stats = sb("stats", [P, NT, 6])
        mv = sb("mv", [P, NT, 2])
        rstd = sb("rstd", [P, 2, NT])
        xn = sb("xn", [P, NT, P])
        xnT = sb("xnT", [P, SEQ])
        qk = sb("qk", [P, 2, QK])
        sq = sb("sq", [P, QK])
        ss = sb("ss", [P, 2, 32])
        rs = sb("rs", [P, 2, 32])
        rotA = sb("rotA", [P, QK])
        rotB = sb("rotB", [P, QK])
        part1 = sb("part1", [P, QK], BF16)
        part2 = sb("part2", [P, QK], BF16)
        part3 = sb("part3", [P, QK], BF16)
        qst = sb("qst", [P, NT, NH, SLOT], BF16)
        kst = sb("kst", [P, NT, 2 * KP, SLOT], BF16)
        qT = sb("qT", [P, 2, 8, SEQ], BF16)
        kT = sb("kT", [P, 2, KP, SEQ], BF16)
        V = sb("V", [P, 2, NT, NV, 32])
        PT = sb("PT", [P, 8, HEAD_COLS])
        oT = sb("oT", [P, SEQ])
        rsum = sb("rsum", [P, NT, 4])
        u = sb("u", [P, NT, 4, VD])
        y = sb("y", [P, NT, P])
        yT = sb("yT", [P, SEQ])
        tmp = sb("tmp", [P, NT, P])
        if gqa:
            bm = sb("bm", [P, NH, 10])
            mx = sb("mx", [P, NT, NH])
            mr = sb("mr", [P, NT, NH])
            mp = sb("mp", [P, NT, NH], BF16)

        S = ctx.enter_context(nc.psum_tensor(A + "S", [P, 2, 1536], F32))
        O = ctx.enter_context(nc.psum_tensor(A + "O", [P, 512], F32))
        M = ctx.enter_context(nc.psum_tensor(A + "M", [P, 512], F32))
        Mb = M[:, :].bitcast(BF16)

        w_loaded = sem("w_loaded")
        w_scaled = sem("w_scaled")
        stats_ready = sem("stats_ready")
        rstd_ready = sem("rstd_ready")
        xn_ready = sem("xn_ready")
        xT_filled = sem("xT_filled")
        xT_copied = sem("xT_copied")
        qkv_filled = sem("qkv_filled")
        qkv_taken = sem("qkv_taken")
        rotA_ready = sem("rotA_ready")
        rotB_ready = sem("rotB_ready")
        stack_ready = sem("stack_ready")
        q_turned = sem("q_turned")
        k_turned = sem("k_turned")
        q_copied = sem("q_copied")
        k_copied = sem("k_copied")
        scores_ready = sem("scores_ready")
        probs_ready = sem("probs_ready")
        av_ready = sem("av_ready")
        o_copied = sem("o_copied")
        o_turned = sem("o_turned")
        o_used = sem("o_used")
        y_ready = sem("y_ready")
        yT_filled = sem("yT_filled")
        yT_copied = sem("yT_copied")
        proj_filled = sem("proj_filled")
        out_done = sem("out_done")
        zeroed = sem("zeroed")
        if gqa:
            stats2_ready = sem("stats2_ready")
            rstd2_ready = sem("rstd2_ready")
            max_filled = sem("max_filled")
            max_used = sem("max_used")
            shift_ready = sem("shift_ready")
            mq_turned = sem("mq_turned")
            mq_copied = sem("mq_copied")
        else:
            x_loaded = sem("x_loaded")
            lam_sums = sem("lam_sums")
            lam_exps = sem("lam_exps")
            ss_ready = sem("ss_ready")
            rs_ready = sem("rs_ready")

        def pe_program(pe):
            def turn_x(c):
                pe.wait_ge(xn_ready, c + 1)
                for t in range(NT):
                    last = pe.transpose(M[:, t * P:(t + 1) * P], xn[:, t, :], C["ident"][:, :])
                last.then_inc(xT_filled, 1)

            def qkv(c, t):
                if t == 0:
                    pe.wait_ge(xT_copied, c + 1)
                else:
                    pe.wait_ge(qkv_taken, NT * c + t)
                pe.matmul(M[:, 0:QKV], xnT[:, t * P:(t + 1) * P], wqkv[:, :], start=True,
                          stop=True).then_inc(qkv_filled, 1)

            def turn_q(c, t):
                for p in range(8):
                    last = pe.transpose(Mb[:, p * P:(p + 1) * P], qst[:, t, 2 * p:2 * p + 2, :],
                                        C["identb"][:, :])
                last.then_inc(q_turned, 1)

            def turn_k(c, t):
                pe.wait_ge(q_copied, NT * c + t + 1)
                for p in range(KP):
                    last = pe.transpose(Mb[:, p * P:(p + 1) * P], kst[:, t, 2 * p:2 * p + 2, :],
                                        C["identb"][:, :])
                last.then_inc(k_turned, 1)

            def scores(b, par, s):
                qp, kp, r, _ = head(s)
                sl = S[:, s % 2, :]
                q, k = qT[r:r + KROWS, par, qp, :], kT[r:r + KROWS, par, kp, :]
                pe.matmul(sl[:, 0:512], C["identb"][:, :], C["maskT"][:, :], start=True, stop=False,
                          skip_group_check=True)
                for j in range(NT):
                    pe.matmul(sl[:, j * P:(j + 1) * P], k[:, j * P:(j + 1) * P],
                              q[:, j * P:(j + 1) * P], start=False, stop=(j == NT - 1),
                              skip_group_check=True)
                for j, (o, n) in OFF_DIAG.items():
                    last = pe.matmul(sl[:, o:o + n], k[:, j * P:(j + 1) * P], q[:, SEQ - n:SEQ],
                                     start=True, stop=True, skip_group_check=True)
                last.then_inc(scores_ready, 1)

            def weigh(b, par, g, part):
                for r in ((0, 1), (2, 3), (4, 5), (6,))[part]:
                    j, off = r // 2, r % 2
                    for c in range(4):
                        vh = head(4 * g + c)[3]
                        pt = PT[:, (4 * g + c) % 8, :]
                        if off:
                            o, n = OFF_DIAG[j]
                            rhs, q0 = pt[:, o:o + n], SEQ - n
                        else:
                            n, q0 = P, j * P
                            rhs = pt[:, j * P:(j + 1) * P]
                        last = pe.matmul(O[32 * c:32 * c + 32, q0:q0 + n], V[:, par, j, vh, :], rhs,
                                         start=(r == 0), stop=(r == 6), skip_group_check=True)
                if part == 3:
                    last.then_inc(av_ready, 1)

            def turn_o(b, g):
                pe.wait_ge(o_copied, 4 * b + g + 1)
                for t in range(NT):
                    last = pe.transpose(M[:, t * P:(t + 1) * P], oT[:, t * P:(t + 1) * P],
                                        C["ident"][:, :])
                last.then_inc(o_turned, 1)

            def prologue():
                pe.wait_ge(w_scaled, 1)
                pe.wait_ge(zeroed, 1)
                turn_x(0)
                for t in range(NT):
                    qkv(0, t)
                pe.wait_ge(qkv_taken, NT)
                for t in range(NT):
                    pe.wait_ge(stack_ready, t + 1)
                    if t:
                        pe.wait_ge(k_copied, t)
                    turn_q(0, t)
                    turn_k(0, t)
                if not gqa:
                    pe.wait_ge(q_copied, NT)
                    pe.wait_ge(k_copied, NT)
                    scores(0, 0, 0)

            def max_phase(b, par, first):
                if not gqa:
                    return
                pe.wait_ge(q_copied, NT * b + NT)
                pe.wait_ge(k_copied, NT * b + NT)
                if not first:
                    pe.wait_ge(probs_ready, NH * b)
                for h in range(NH):
                    if h >= 2:
                        pe.wait_ge(max_used, NH * b + h - 1)
                    qp, kp, r, _ = head(h)
                    sl = S[:, h % 2, :]
                    q, k = qT[r:r + 48, par, qp, :], kT[r:r + 48, par, kp, :]
                    pe.matmul(sl[:, 0:512], C["identb"][:, :], C["maskQ"][:, :], start=True,
                              stop=False, skip_group_check=True)
                    for j in range(NT):
                        pe.matmul(sl[:, j * P:(j + 1) * P], q[:, j * P:(j + 1) * P],
                                  k[:, j * P:(j + 1) * P], start=False, stop=(j == NT - 1),
                                  skip_group_check=True)
                    for i, o in ((3, 512), (1, 896), (2, 1024)):
                        last = pe.matmul(sl[:, o:o + i * P], q[:, i * P:(i + 1) * P], k[:, 0:i * P],
                                         start=True, stop=True, skip_group_check=True)
                    last.then_inc(max_filled, 1)
                pe.wait_ge(max_used, NH * b + NH)
                pe.wait_ge(shift_ready, b + 1)
                for t in range(NT):
                    bank = S[:, t // 2, (t % 2) * 512:(t % 2) * 512 + 512].bitcast(BF16)
                    for p in range(8):
                        last = pe.transpose(bank[:, p * P:(p + 1) * P],
                                            qst[:, t, 2 * p:2 * p + 2, :], C["identb"][:, :])
                    last.then_inc(mq_turned, 1)
                pe.wait_ge(mq_copied, NT * b + NT)
                scores(b, par, 0)

            def attend(b, par, first, last_b):
                c = b + 1
                for s in range(NH):
                    if s < NH - 1:
                        if s >= 1 or not (first or gqa):
                            pe.wait_ge(probs_ready, NH * b + s)
                        scores(b, par, s + 1)
                    elif not last_b and not gqa:
                        pe.wait_ge(probs_ready, NH * b + s)
                        pe.wait_ge(q_copied, NT * c + NT)
                        pe.wait_ge(k_copied, NT * c + NT - 1)
                    g, part = s // 4 - 1, s % 4
                    if g >= 0:
                        if part == 0:
                            pe.wait_ge(probs_ready, NH * b + 4 * g + 4)
                            if not (first and g == 0):
                                pe.wait_ge(o_copied, 4 * b + g)
                        weigh(b, par, g, part)
                    if not last_b:
                        if s == 0:
                            pe.wait_ge(k_copied, NT * c)
                            if not first:
                                pe.wait_ge(out_done, b)
                            turn_x(c)
                        if 1 <= s <= 4:
                            qkv(c, s - 1)
                        for t, at in enumerate((6, 9, 11, 14)):
                            if s == at:
                                if t == 0:
                                    pe.wait_ge(qkv_taken, NT * c + NT)
                                elif t == 1:
                                    pe.wait_ge(o_used, 4 * b + 1)
                                else:
                                    pe.wait_ge(k_copied, NT * c + t)
                                pe.wait_ge(stack_ready, NT * c + t + 1)
                                turn_q(c, t)
                        for t, at in enumerate((7, 10, 13, 15)):
                            if s == at:
                                if t == 2:
                                    pe.wait_ge(o_used, 4 * b + 2)
                                turn_k(c, t)
                    if s == 8:
                        if not last_b:
                            pe.wait_ge(k_copied, NT * c + 1)
                        elif not first:
                            pe.wait_ge(out_done, b)
                        turn_o(b, 0)
                    if s == 12:
                        if not last_b:
                            pe.wait_ge(q_copied, NT * c + 3)
                        else:
                            pe.wait_ge(o_used, 4 * b + 1)
                        turn_o(b, 1)
                if not last_b and not gqa:
                    pe.wait_ge(k_copied, NT * c + NT)
                    scores(c, 1 - par, 0)
                pe.wait_ge(probs_ready, NH * b + NH)
                pe.wait_ge(o_copied, 4 * b + 3)
                for part in range(4):
                    weigh(b, par, 3, part)
                if not last_b:
                    pe.wait_ge(k_copied, NT * c + NT)
                pe.wait_ge(o_used, 4 * b + 2)
                turn_o(b, 2)
                pe.wait_ge(o_used, 4 * b + 3)
                turn_o(b, 3)
                pe.wait_ge(y_ready, b + 1)
                for t in range(NT):
                    last = pe.transpose(M[:, t * P:(t + 1) * P], y[:, t, :], C["ident"][:, :])
                last.then_inc(yT_filled, 1)
                pe.wait_ge(yT_copied, b + 1)
                for t in range(NT):
                    last = pe.matmul(M[:, t * P:(t + 1) * P], yT[:, t * P:(t + 1) * P], wout[:, :],
                                     start=(t == 0), stop=(t == NT - 1), skip_group_check=True)
                last.then_inc(proj_filled, 1)

            return prologue, max_phase, attend

        def act_program(act):
            def copy_xT(c):
                act.wait_ge(xT_filled, c + 1)
                act.activation(xnT[:, :], M[:, :], ACT.Copy).then_inc(xT_copied, 1)

            def take_qkv(c, par, t):
                act.wait_ge(qkv_filled, NT * c + t + 1)
                if not (isinstance(c, int) and c == 0 and t < 2):
                    act.wait_ge(stack_ready, NT * c + t - 1)
                act.activation(qk[:, t % 2, :], M[:, 0:QK], ACT.Copy)
                act.activation(V[:, par, t, :, 0:VD],
                               M[:, QK:QKV].rearrange("p (h d) -> p h d", d=VD),
                               ACT.Copy).then_inc(qkv_taken, 1)

            def rms(c, t):
                if gqa:
                    return
                act.wait_ge(ss_ready, NT * c + t + 1)
                act.activation(rs[:, t % 2, :], ss[:, t % 2, :], ACT.Ln, scale=1.0 / HD,
                               bias=C["rms_eps"][:, 0:1])
                act.drain()
                act.activation(rs[:, t % 2, :], rs[:, t % 2, :], ACT.Exp, scale=-0.5
                               ).then_inc(rs_ready, 1)

            def copy_k(c, par, t):
                act.wait_ge(k_turned, NT * c + t + 1)
                act.activation(kT[:, par, :, t * P:(t + 1) * P],
                               Mb[:, 0:KP * P].rearrange("r (p n) -> r p n", n=P), ACT.Copy
                               ).then_inc(k_copied, 1)

            def prologue():
                act.preload_act_table_set("natural_log_exp_and_others")
                act.wait_ge(zeroed, 1)
                if not gqa:
                    act.wait_ge(lam_sums, 1)
                    act.activation(lam_s[:, 2:4], lam_s[:, 0:2], ACT.Exp).then_inc(lam_exps, 1)
                copy_xT(0)
                for t in range(NT):
                    take_qkv(0, 0, t)
                    rms(0, t)
                for t in range(NT):
                    copy_k(0, 0, t)

            def max_phase(b, par, first):
                if not gqa:
                    return
                for t in range(NT):
                    act.wait_ge(mq_turned, NT * b + t + 1)
                    bank = S[:, t // 2, (t % 2) * 512:(t % 2) * 512 + 512].bitcast(BF16)
                    act.activation(qT[:, par, :, t * P:(t + 1) * P],
                                   bank.rearrange("r (p n) -> r p n", n=P), ACT.Copy
                                   ).then_inc(mq_copied, 1)

            def attend(b, par, first, last_b):
                c = b + 1
                for s in range(NH):
                    act.wait_ge(scores_ready, NH * b + s + 1)
                    if s % 4 == 0 and not (first and s < 8):
                        act.wait_ge(av_ready, 4 * b + s // 4 - 1)
                    act.activation(PT[:, s % 8, :], S[:, s % 2, 0:HEAD_COLS], ACT.Exp, scale=SCALE
                                   ).then_inc(probs_ready, 1)
                    if not last_b:
                        if s == 1:
                            if not first:
                                act.wait_ge(av_ready, 4 * b)
                            copy_xT(c)
                        if 2 <= s <= 5:
                            take_qkv(c, 1 - par, s - 2)
                        if 3 <= s <= 6:
                            rms(c, s - 3)
                        for t, at in enumerate((8, 11, 14)):
                            if s == at:
                                copy_k(c, 1 - par, t)
                if not last_b:
                    copy_k(c, 1 - par, 3)
                act.wait_ge(yT_filled, b + 1)
                act.activation(yT[:, :], M[:, :], ACT.Copy).then_inc(yT_copied, 1)

            return prologue, max_phase, attend

        def pool_program(pool):
            def rsqrt_stats(c):
                pool.wait_ge(stats_ready, c + 1)
                pool.tensor_tensor(rstd[:, 0, :], mv[:, :, 1], C["ln_eps"][:, :], ALU.add)
                pool.drain()
                pool.tensor_tensor(rstd[:, 0, :], rstd[:, 0, :], C["half"][:, 0:NT], ALU.pow
                                   ).then_inc(rstd_ready, 1)
                if gqa:
                    pool.wait_ge(stats2_ready, c + 1)
                    pool.tensor_tensor(rstd[:, 1, :], mv[:, :, 0], mv[:, :, 0], ALU.mult)
                    pool.drain()
                    pool.tensor_tensor(rstd[:, 1, :], rstd[:, 1, :], mv[:, :, 1], ALU.add)
                    pool.drain()
                    pool.tensor_scalar(rstd[:, 1, :], rstd[:, 1, :], LN_EPS, None, ALU.add)
                    pool.drain()
                    pool.tensor_tensor(rstd[:, 1, :], rstd[:, 1, :], C["half"][:, 0:NT], ALU.pow
                                       ).then_inc(rstd2_ready, 1)

            def rotate_b(c, t):
                pool.wait_ge(qkv_taken, NT * c + t + 1)
                if not (isinstance(c, int) and c == 0 and t == 0):
                    pool.wait_ge(rotA_ready, NT * c + t)
                x = qk[:, t % 2, :].rearrange("p (h a d) -> p h a d", a=2, d=4)
                for a in range(2):
                    last = pool.tensor_tensor(
                        rotB[:, :].rearrange("p (h a d) -> p h a d", a=2, d=4)[:, :, a, :],
                        x[:, :, 1 - a, :],
                        C["sin"][:, t, 4 * a:4 * a + 4].unsqueeze(1).to_broadcast([P, NHK, 4]),
                        ALU.mult)
                last.then_inc(rotB_ready, 1)

            def prologue():
                rsqrt_stats(0)
                for t in range(NT):
                    rotate_b(0, t)

            def attend(b, par, first, last_b):
                if not last_b:
                    rsqrt_stats(b + 1)
                    for t in range(NT):
                        rotate_b(b + 1, t)

            return prologue, lambda b, par, first: None, attend

        def dve_program(v):
            def normalise(c):
                if not gqa:
                    v.wait_ge(x_loaded, 16 * (c + 1))
                if not (isinstance(c, int) and c == 0):
                    v.wait_ge(xT_filled, c)
                for t in range(NT):
                    v.bn_stats(stats[:, t, :], tile_of(XT, c, t))
                v.drain()
                for t in range(NT):
                    last = v.bn_aggr(mv[:, t, :], stats[:, t, :])
                last.then_inc(stats_ready, 1)
                v.wait_ge(rstd_ready, c + 1)
                if not gqa:
                    for t in range(NT):
                        last = v.tensor_scalar(xn[:, t, :], tile_of(XT, c, t), mv[:, t, 0:1],
                                               rstd[:, 0, t:t + 1], ALU.subtract, ALU.mult)
                    last.then_inc(xn_ready, 1)
                    return
                v.wait_ge(stats_ready, c + 1)
                for t in range(NT):
                    v.tensor_scalar(tile_of(OUT, c, t), tile_of(XT, c, t), mv[:, t, 0:1],
                                    rstd[:, 0, t:t + 1], ALU.subtract, ALU.mult)
                v.drain()
                for t in range(NT):
                    v.bn_stats(stats[:, t, :], tile_of(OUT, c, t))
                v.drain()
                for t in range(NT):
                    last = v.bn_aggr(mv[:, t, :], stats[:, t, :])
                last.then_inc(stats2_ready, 1)
                v.wait_ge(rstd2_ready, c + 1)
                for t in range(NT):
                    last = v.tensor_scalar(xn[:, t, :], tile_of(OUT, c, t), rstd[:, 1, t:t + 1],
                                           None, ALU.mult)
                last.then_inc(xn_ready, 1)

            def squares(c, t):
                if gqa:
                    return
                v.wait_ge(qkv_taken, NT * c + t + 1)
                v.tensor_tensor(sq[:, :], qk[:, t % 2, :], qk[:, t % 2, :], ALU.mult)
                v.drain()
                v.tensor_reduce(ss[:, t % 2, :], sq[:, :].rearrange("p (h d) -> p h d", d=HD), AX.X,
                                ALU.add).then_inc(ss_ready, 1)

            def stack(c, t):
                v.wait_ge(qkv_taken, NT * c + t + 1)
                x = qk[:, t % 2, :].rearrange("p (h d) -> p h d", d=HD)
                a = rotA[:, :].rearrange("p (h d) -> p h d", d=HD)
                v.tensor_tensor(a, x, C["cos"][:, t, :].unsqueeze(1).to_broadcast([P, NHK, HD]),
                                ALU.mult)
                v.drain()
                v.wait_ge(rotB_ready, NT * c + t + 1)
                v.tensor_tensor(rotA[:, :], rotA[:, :], rotB[:, :], ALU.add
                                ).then_inc(rotA_ready, 1)
                v.drain()
                if not gqa:
                    v.wait_ge(rs_ready, NT * c + t + 1)
                    v.tensor_tensor(a, a, rs[:, t % 2, :].unsqueeze(2).to_broadcast([P, NHK, HD]),
                                    ALU.mult)
                    v.drain()
                v.tensor_copy(part1[:, :], rotA[:, :])
                v.drain()
                v.tensor_tensor(rotB2[:, :], rotA[:, :], part1[:, :], ALU.subtract)
                v.drain()
                v.tensor_copy(part2[:, :], rotB2[:, :])
                v.drain()
                v.tensor_tensor(part3[:, :], rotB2[:, :], part2[:, :], ALU.subtract)
                v.drain()
                if not (isinstance(c, int) and c == 0):
                    v.wait_ge(q_turned, NT * c + t - 3)
                    v.wait_ge(k_turned, NT * c + t - 3)
                def parts(p, lo, n):
                    return p[:, lo * HD:(lo + n) * HD].rearrange("p (h d) -> p h d", d=HD)

                def rep(ap, n, k):
                    return ap.unsqueeze(2).to_broadcast([P, n, k, HD])

                q = qst[:, t, :, 0:48].rearrange("p h (s d) -> p h s d", d=HD)
                v.tensor_copy(q[:, :, 0:3, :], rep(parts(part1, 0, NH), NH, 3))
                v.tensor_copy(q[:, :, 3:5, :], rep(parts(part2, 0, NH), NH, 2))
                v.tensor_copy(q[:, :, 5, :], parts(part3, 0, NH))
                if gqa:
                    kv = kst[:, t, :, 0:48].rearrange("p (g e) (s d) -> p g e s d", e=2, d=HD)
                    for e in range(2):
                        for slot, p in enumerate((part1, part2, part3, part1, part2, part1)):
                            last = v.tensor_copy(kv[:, :, e, slot, :], parts(p, NH, NK))
                else:
                    k = kst[:, t, :, 0:48].rearrange("p h (s d) -> p h s d", d=HD)
                    v.tensor_copy(k[:, :, 0:4:3, :], rep(parts(part1, NH, NK), NK, 2))
                    v.tensor_copy(k[:, :, 5, :], parts(part1, NH, NK))
                    v.tensor_copy(k[:, :, 1:5:3, :], rep(parts(part2, NH, NK), NK, 2))
                    last = v.tensor_copy(k[:, :, 2, :], parts(part3, NH, NK))
                last.then_inc(stack_ready, 1)

            def copy_q(c, par, t):
                v.wait_ge(q_turned, NT * c + t + 1)
                v.tensor_copy(qT[:, par, :, t * P:(t + 1) * P],
                              Mb.rearrange("r (p n) -> r p n", n=P)).then_inc(q_copied, 1)

            def copy_o(b, g):
                v.wait_ge(av_ready, 4 * b + g + 1)
                if not (isinstance(b, int) and b == 0 and g == 0):
                    v.wait_ge(o_turned, 4 * b + g)
                v.tensor_copy(oT[:, :], O[:, :]).then_inc(o_copied, 1)

            def combine(b, g):
                v.wait_ge(o_turned, 4 * b + g + 1)
                o = M[:, :].rearrange("p (t c d) -> p t c d", t=NT, c=4)
                v.reciprocal(rsum[:, :, :], o[:, :, :, VD])
                v.drain()
                if gqa:
                    if g == 0 and not (isinstance(b, int) and b == 0):
                        v.wait_ge(yT_filled, b)
                    for t in range(NT):
                        last = v.tensor_tensor(
                            y[:, t, 32 * g:32 * g + 32].rearrange("p (c d) -> p c d", c=4),
                            o[:, t, :, 0:VD], rsum[:, t, :].unsqueeze(2).to_broadcast([P, 4, VD]),
                            ALU.mult)
                    last.then_inc(o_used, 1)
                    if g == 3:
                        v.wait_ge(o_used, 4 * b + 4)
                        v.sem_inc(y_ready, 1)
                    return
                v.tensor_scalar(rsum[:, :, 2:4], rsum[:, :, 2:4], lam_s[:, 6:7], None, ALU.mult)
                v.drain()
                for t in range(NT):
                    last = v.tensor_tensor(u[:, t, :, :], o[:, t, :, 0:VD],
                                           rsum[:, t, :].unsqueeze(2).to_broadcast([P, 4, VD]),
                                           ALU.mult)
                last.then_inc(o_used, 1)
                v.wait_ge(o_used, 4 * b + g + 1)
                if g == 0 and not (isinstance(b, int) and b == 0):
                    v.wait_ge(yT_filled, b)
                last = v.tensor_tensor(
                    y[:, :, 32 * g:32 * g + 32].rearrange("p t (c d) -> p t c d", c=2),
                    u[:, :, 0:2, :], u[:, :, 2:4, :], ALU.add)
                if g == 3:
                    last.then_inc(y_ready, 1)
                else:
                    v.drain()

            def add_out(b):
                v.wait_ge(proj_filled, b + 1)
                m = M[:, :].rearrange("p (t d) -> p t d", t=NT)
                if gqa:
                    v.tensor_tensor(tmp[:, :, :], m, OUT[:, ds(4 * b, 4), :], ALU.add)
                    v.drain()
                    v.tensor_scalar(OUT[:, ds(4 * b, 4), :], tmp[:, :, :], 100.0, -100.0, ALU.min,
                                    ALU.max).then_inc(out_done, 1)
                else:
                    v.tensor_tensor(XT[:, ds(4 * b, 4), :], m, XT[:, ds(4 * b, 4), :],
                                    ALU.add).then_inc(out_done, 1)

            def prologue():
                v.memset(qst[:, :, :, :], 0.0)
                v.memset(kst[:, :, :, :], 0.0)
                v.memset(V[:, :, :, :, :], 0.0)
                v.drain()
                v.memset(kst[:, :, :, 48:51], 1.0)
                v.memset(V[:, :, :, :, VD:VD + 1], 1.0).then_inc(zeroed, 1)
                v.wait_ge(w_loaded, C["stage_loads"])
                if gqa:
                    v.tensor_scalar(wqkv[:, :], wqkv[:, :], lnw[:, 0:1], None, ALU.mult
                                    ).then_inc(w_scaled, 1)
                else:
                    v.tensor_tensor(lam[:, 0, :], lam[:, 0, :], lam[:, 1, :], ALU.mult)
                    v.tensor_tensor(lam[:, 2, :], lam[:, 2, :], lam[:, 3, :], ALU.mult)
                    v.drain()
                    v.tensor_reduce(lam_s[:, 0:2], lam[:, 0:4:2, :], AX.X, ALU.add
                                    ).then_inc(lam_sums, 1)
                    v.wait_ge(lam_exps, 1)
                    v.tensor_scalar(lam_s[:, 4:5], lam_s[:, 2:3], -1.0, None, ALU.mult)
                    v.drain()
                    v.tensor_tensor(lam_s[:, 5:6], lam_s[:, 3:4], lam_s[:, 4:5], ALU.add)
                    v.drain()
                    v.tensor_scalar(lam_s[:, 6:7], lam_s[:, 5:6], -C["lambda_init"], None,
                                    ALU.add).then_inc(w_scaled, 1)
                normalise(0)
                for t in range(NT):
                    squares(0, t)
                    stack(0, t)
                for t in range(NT):
                    copy_q(0, 0, t)

            def max_phase(b, par, first):
                if not gqa:
                    return
                for h in range(NH):
                    v.wait_ge(max_filled, NH * b + h + 1)
                    v.tensor_reduce(bm[:, h, :],
                                    S[:, h % 2, 0:HEAD_COLS].rearrange("p (k n) -> p k n", n=P),
                                    AX.X, ALU.max).then_inc(max_used, 1)
                v.drain()
                v.tensor_copy(mx[:, 0, :], bm[:, :, 0])
                v.tensor_tensor(mx[:, 1, :], bm[:, :, 1], bm[:, :, 7], ALU.max)
                v.tensor_tensor(mx[:, 2, :], bm[:, :, 2], bm[:, :, 8], ALU.max)
                v.tensor_reduce(mx[:, 3, :], bm[:, :, 3:7], AX.X, ALU.max)
                v.drain()
                v.tensor_tensor(mx[:, 2, :], mx[:, 2, :], bm[:, :, 9], ALU.max)
                v.drain()
                v.tensor_scalar(mx[:, :, :], mx[:, :, :], -1.0, None, ALU.mult)
                v.drain()
                for i in range(3):
                    v.tensor_copy(mp[:, :, :], mx[:, :, :])
                    v.drain()
                    last = v.tensor_copy(qst[:, :, :, 48 + i], mp[:, :, :])
                    if i < 2:
                        v.tensor_tensor(mx[:, :, :], mx[:, :, :], mp[:, :, :], ALU.subtract)
                        v.drain()
                last.then_inc(shift_ready, 1)

            def attend(b, par, first, last_b):
                c = b + 1
                if not last_b:
                    normalise(c)
                    for t in range(NT):
                        squares(c, t)
                        stack(c, t)
                    copy_q(c, 1 - par, 0)
                copy_o(b, 0)
                combine(b, 0)
                if not last_b:
                    copy_q(c, 1 - par, 1)
                    copy_q(c, 1 - par, 2)
                copy_o(b, 1)
                combine(b, 1)
                if not last_b:
                    copy_q(c, 1 - par, 3)
                for g in (2, 3):
                    copy_o(b, g)
                    if g == 2:
                        combine(b, 2)
                combine(b, 3)
                add_out(b)

            rotB2 = sq
            return prologue, max_phase, attend

        def run(eng, program):
            prologue, max_phase, attend = program(eng)
            prologue()
            max_phase(0, 0, True)
            attend(0, 0, True, False)
            if NB > 2:
                max_phase(1, 1, False)
                attend(1, 1, False, False)
                with eng.Fori(1, NB // 2 - 1) as pair:
                    for par in range(2):
                        b = 2 * pair + par
                        max_phase(b, par, False)
                        attend(b, par, False, False)
                max_phase(NB - 2, 0, False)
                attend(NB - 2, 0, False, False)
            max_phase(NB - 1, 1, False)
            attend(NB - 1, 1, False, True)

        with nc.Block() as block:
            @block.sync
            def _(sp):
                sp.dma_start(wqkv[:, :], C["wqkv_dram"]).then_inc(w_loaded, 16)
                sp.dma_start(wout[:, :], C["wout_dram"]).then_inc(w_loaded, 16)
                if gqa:
                    sp.dma_start(lnw[:, 0:1], C["ln1w_dram"]).then_inc(w_loaded, 16)
                else:
                    for i in range(4):
                        sp.dma_start(lam[:, i, :], C["lam_dram"][i].unsqueeze(0).to_broadcast([P, 4])
                                     ).then_inc(w_loaded, 16)
                    for b in range(NB):
                        if b:
                            sp.wait_ge(x_loaded, 16 * b)
                        sp.dma_start(XT[:, 4 * b:4 * b + 4, :], C["x_dram"][b].rearrange(
                            "(t p) d -> p t d", p=P)).then_inc(x_loaded, 16)

            @block.tensor
            def _(pe):
                run(pe, pe_program)

            @block.scalar
            def _(act):
                run(act, act_program)

            @block.gpsimd
            def _(pool):
                run(pool, pool_program)

            @block.vector
            def _(v):
                run(v, dve_program)


def pairs_of_batches(eng, NB, step):
    step(0, 0, True, False)
    step(1, 1, False, False)
    with eng.Fori(1, NB // 2 - 1) as pair:
        for par in range(2):
            step(2 * pair + par, par, False, False)
    step(NB - 2, 0, False, False)
    step(NB - 1, 1, False, True)


def expert_stage(nc, C, XT, H, NB):
    E, F = 8, 256
    FC = F // P

    with ExitStack() as ctx:
        def sb(name, shape, dt=F32):
            return ctx.enter_context(nc.sbuf_tensor("moe_" + name, shape, dt))

        def ps(name, shape, dt=F32):
            return ctx.enter_context(nc.psum_tensor("moe_" + name, shape, dt))

        def sem(name):
            return C["sems"].enter_context(nc.semaphore("moe_" + name))

        wg = sb("wg", [P, E, F])
        wu = sb("wu", [P, E, F])
        wd = sb("wd", [P, E, FC, P])
        wr = sb("wr", [P, E])
        lnw = sb("lnw", [P, 1])
        stats = sb("stats", [P, NT, 6])
        mv = sb("mv", [P, NT, 2])
        rstd = sb("rstd", [P, NT])
        hn = sb("hn", [P, NT, P])
        hT = sb("hT", [P, 2, SEQ])
        sg = sb("sg", [P, 2, SEQ])
        aT = sb("aT", [P, 2, FC, SEQ])
        acc = sb("acc", [P, NT, P])
        top = sb("top", [P, NT, 8])
        topi = sb("topi", [P, NT, 8], mybir.dt.uint32)
        topf = sb("topf", [P, NT, 2])
        logit = sb("logit", [P, NT, E])
        ex = sb("ex", [P, NT, E])
        pick = sb("pick", [P, NT, E])
        pick2 = sb("pick2", [P, NT, E])
        esum = sb("esum", [P, NT])
        wt = sb("wt", [P, 2, NT, E])

        GU = ps("GU", [P, 2, 2, 512])
        D = ps("D", [P, 2, 512])
        M = ps("M", [P, 512])

        w_loaded = sem("w_loaded")
        w_scaled = sem("w_scaled")
        stats_ready = sem("stats_ready")
        rstd_ready = sem("rstd_ready")
        hn_ready = sem("hn_ready")
        hT_filled = sem("hT_filled")
        hT_copied = sem("hT_copied")
        route_filled = sem("route_filled")
        logits_taken = sem("logits_taken")
        top_ready = sem("top_ready")
        ex_ready = sem("ex_ready")
        gu_filled = sem("gu_filled")
        silu_ready = sem("silu_ready")
        a_ready = sem("a_ready")
        down_filled = sem("down_filled")
        acc_done = sem("acc_done")

        def pe_program(pe):
            def turn(c):
                pe.wait_ge(hn_ready, c + 1)
                for t in range(NT):
                    last = pe.transpose(M[:, t * P:(t + 1) * P], hn[:, t, :], C["ident"][:, :])
                last.then_inc(hT_filled, 1)

            def route(c, par):
                pe.wait_ge(hT_copied, c + 1)
                for t in range(NT):
                    last = pe.matmul(M[:, t * E:(t + 1) * E], hT[:, par, t * P:(t + 1) * P],
                                     wr[:, :], start=(t == 0), stop=(t == NT - 1),
                                     skip_group_check=True)
                last.then_inc(route_filled, 1)

            def down(b, e, first):
                pe.wait_ge(a_ready, FC * (E * b + e) + FC)
                if not (first and e < 2):
                    pe.wait_ge(acc_done, E * b + e - 1)
                i = e % 2
                for t in range(NT):
                    for f in range(FC):
                        last = pe.matmul(D[:, i, t * P:(t + 1) * P],
                                         aT[:, i, f, t * P:(t + 1) * P], wd[:, e, f, :],
                                         start=(t == 0 and f == 0), stop=(f == FC - 1),
                                         skip_group_check=True)
                last.then_inc(down_filled, 1)

            def step(b, par, first, last_b):
                for e in range(E):
                    for f in range(FC):
                        if not (first and e == 0):
                            pe.wait_ge(a_ready, FC * (E * b + e) + f - 1)
                        elif f == 0:
                            pe.wait_ge(hT_copied, 1)
                        pe.matmul(GU[:, f, 0, :], wg[:, e, f * P:(f + 1) * P], hT[:, par, :],
                                  start=True, stop=True)
                        pe.matmul(GU[:, f, 1, :], wu[:, e, f * P:(f + 1) * P], hT[:, par, :],
                                  start=True, stop=True).then_inc(gu_filled, 1)
                    if e:
                        down(b, e - 1, first)
                    if not last_b and e == 2:
                        pe.wait_ge(logits_taken, b + 1)
                        turn(b + 1)
                    if not last_b and e == 4:
                        route(b + 1, 1 - par)
                down(b, E - 1, first)

            pe.wait_ge(w_scaled, 1)
            turn(0)
            route(0, 0)
            pairs_of_batches(pe, NB, step)

        def act_program(act):
            def exps(c):
                act.wait_ge(top_ready, c + 1)
                act.activation(ex[:, :, :], ex[:, :, :], ACT.Exp).then_inc(ex_ready, 1)

            def copy_hT(c, par):
                act.wait_ge(hT_filled, c + 1)
                act.activation(hT[:, par, :], M[:, :], ACT.Copy).then_inc(hT_copied, 1)

            def step(b, par, first, last_b):
                for e in range(E):
                    for f in range(FC):
                        n = FC * (E * b + e) + f
                        act.wait_ge(gu_filled, n + 1)
                        if not (first and e == 0):
                            act.wait_ge(a_ready, n - 1)
                        act.activation(sg[:, f, :], GU[:, f, 0, :], ACT.Silu
                                       ).then_inc(silu_ready, 1)
                    if not last_b and e == 3:
                        copy_hT(b + 1, 1 - par)
                    if not last_b and e == 5:
                        exps(b + 1)

            copy_hT(0, 0)
            exps(0)
            pairs_of_batches(act, NB, step)

        def pool_program(pool):
            def rsqrt_stats(c):
                pool.wait_ge(stats_ready, c + 1)
                pool.tensor_tensor(rstd[:, :], mv[:, :, 0], mv[:, :, 0], ALU.mult)
                pool.drain()
                pool.tensor_tensor(rstd[:, :], rstd[:, :], mv[:, :, 1], ALU.add)
                pool.drain()
                pool.tensor_scalar(rstd[:, :], rstd[:, :], LN_EPS, None, ALU.add)
                pool.drain()
                pool.tensor_tensor(rstd[:, :], rstd[:, :], C["half"][:, 0:NT], ALU.pow
                                   ).then_inc(rstd_ready, 1)

            def step(b, par, first, last_b):
                if not last_b:
                    rsqrt_stats(b + 1)

            rsqrt_stats(0)
            pairs_of_batches(pool, NB, step)

        def dve_program(v):
            def normalise(c):
                for t in range(NT):
                    v.bn_stats(stats[:, t, :], tile_of(H, c, t))
                v.drain()
                for t in range(NT):
                    last = v.bn_aggr(mv[:, t, :], stats[:, t, :])
                last.then_inc(stats_ready, 1)
                v.wait_ge(rstd_ready, c + 1)
                if not (isinstance(c, int) and c == 0):
                    v.wait_ge(hT_filled, c)
                for t in range(NT):
                    last = v.tensor_scalar(hn[:, t, :], tile_of(H, c, t), rstd[:, t:t + 1], None,
                                           ALU.mult)
                last.then_inc(hn_ready, 1)

            def choose(c):
                v.wait_ge(route_filled, c + 1)
                v.tensor_copy(logit[:, :, :], M[:, 0:NT * E].rearrange("p (t e) -> p t e", t=NT)
                              ).then_inc(logits_taken, 1)
                v.drain()
                for t in range(NT):
                    v.max(top[:, t, :], logit[:, t, :])
                v.drain()
                for t in range(NT):
                    v.max_index(topi[:, t, :], top[:, t, :], logit[:, t, :])
                v.tensor_tensor(ex[:, :, :], logit[:, :, :],
                                top[:, :, 0:1].to_broadcast([P, NT, E]), ALU.subtract
                                ).then_inc(top_ready, 1)

            def weights(c, par):
                v.wait_ge(ex_ready, c + 1)
                v.tensor_copy(topf[:, :, :], topi[:, :, 0:2])
                v.drain()
                for i, o in enumerate((pick, pick2)):
                    v.tensor_tensor(o[:, :, :], C["iota8"][:, :].unsqueeze(1).to_broadcast([P, NT, E]),
                                    topf[:, :, i:i + 1].to_broadcast([P, NT, E]), ALU.is_equal)
                v.drain()
                v.tensor_tensor(pick[:, :, :], pick[:, :, :], pick2[:, :, :], ALU.add)
                v.drain()
                v.tensor_tensor(pick[:, :, :], pick[:, :, :], ex[:, :, :], ALU.mult)
                v.drain()
                v.tensor_reduce(esum[:, :], pick[:, :, :], AX.X, ALU.add)
                v.drain()
                v.reciprocal(esum[:, :], esum[:, :])
                v.drain()
                v.tensor_tensor(wt[:, par, :, :], pick[:, :, :],
                                esum[:, :].unsqueeze(2).to_broadcast([P, NT, E]), ALU.mult)
                v.drain()

            def accumulate(b, par, e):
                v.wait_ge(down_filled, E * b + e + 1)
                if e:
                    v.wait_ge(acc_done, E * b + e)
                for t in range(NT):
                    last = v.scalar_tensor_tensor(
                        out=acc[:, t, :], in0=D[:, e % 2, t * P:(t + 1) * P],
                        scalar=wt[:, par, t, e:e + 1],
                        in1=acc[:, t, :] if e else tile_of(H, b, t), op0=ALU.mult, op1=ALU.add)
                last.then_inc(acc_done, 1)

            def step(b, par, first, last_b):
                for e in range(E):
                    for f in range(FC):
                        n = FC * (E * b + e) + f
                        v.wait_ge(silu_ready, n + 1)
                        if not (first and e < 2):
                            v.wait_ge(down_filled, E * b + e - 1)
                        v.tensor_tensor(aT[:, e % 2, f, :], GU[:, f, 1, :], sg[:, f, :], ALU.mult
                                        ).then_inc(a_ready, 1)
                    if e:
                        accumulate(b, par, e - 1)
                    if not last_b:
                        if e == 1:
                            normalise(b + 1)
                        if e == 5:
                            choose(b + 1)
                        if e == 6:
                            weights(b + 1, 1 - par)
                accumulate(b, par, E - 1)
                v.drain()
                v.tensor_scalar(acc[:, :, :], acc[:, :, :], 100.0, -100.0, ALU.min, ALU.max)
                v.drain()
                x = XT[:, ds(4 * b, 4), :]
                v.tensor_tensor(x, x, acc[:, :, :], ALU.add)

            v.wait_ge(w_loaded, 16 * 5)
            v.tensor_scalar(wg[:, :, :], wg[:, :, :], lnw[:, 0:1], None, ALU.mult)
            v.tensor_scalar(wu[:, :, :], wu[:, :, :], lnw[:, 0:1], None, ALU.mult)
            v.tensor_scalar(wr[:, :], wr[:, :], lnw[:, 0:1], None, ALU.mult).then_inc(w_scaled, 1)
            normalise(0)
            choose(0)
            weights(0, 0)
            pairs_of_batches(v, NB, step)

        with nc.Block() as block:
            @block.sync
            def _(sp):
                sp.dma_start(wg[:, :, :], C["wg_dram"]).then_inc(w_loaded, 16)
                sp.dma_start(wu[:, :, :], C["wu_dram"]).then_inc(w_loaded, 16)
                sp.dma_start(wd[:, :, :, :], C["wd_dram"]).then_inc(w_loaded, 16)
                sp.dma_start(wr[:, :], C["wr_dram"]).then_inc(w_loaded, 16)
                sp.dma_start(lnw[:, :], C["ln2w_dram"]).then_inc(w_loaded, 16)

            block.tensor(pe_program)
            block.scalar(act_program)
            block.gpsimd(pool_program)
            block.vector(dve_program)


def ternary_stage(nc, C, XT, NB):
    HID = 512
    KC = HID // P
    R = 16
    MAGIC = 1.5 * 2.0 ** 23

    with ExitStack() as ctx:
        def sb(name, shape, dt=F32):
            return ctx.enter_context(nc.sbuf_tensor("ff_" + name, shape, dt))

        def ps(name, shape, dt=F32):
            return ctx.enter_context(nc.psum_tensor("ff_" + name, shape, dt))

        def sem(name):
            return C["sems"].enter_context(nc.semaphore("ff_" + name))

        wfc = sb("wfc", [P, KC, P])
        wpr = sb("wpr", [P, HID])
        uT = sb("uT", [R, HID])
        fbT = sb("fbT", [R, R])
        vv = sb("vv", [R, P])
        fv = sb("fv", [R, P])
        gate = sb("gate", [P, 1])
        scl = sb("scl", [P, 5])
        rcp = sb("rcp", [P, 5])
        tern = sb("tern", [P, KC, P])
        wfcT = sb("wfcT", [P, KC, P])
        wprT = sb("wprT", [P, KC, P])
        stats = sb("stats", [P, NT, 6])
        mv = sb("mv", [P, NT, 2])
        rstd = sb("rstd", [P, NT])
        xn = sb("xn", [P, NT, P])
        xT = sb("xT", [P, SEQ])
        r1 = sb("r1", [P, KC, SEQ])
        r2 = sb("r2", [P, KC, SEQ])
        yo = sb("yo", [P, 2, NT, P])

        HB = ps("HB", [P, KC, 512])
        Y = ps("Y", [P, 2, 512])
        M = ps("M", [P, 512])

        w_loaded = sem("w_loaded")
        fv_filled = sem("fv_filled")
        fv_copied = sem("fv_copied")
        low_filled = sem("low_filled")
        wfc_ready = sem("wfc_ready")
        wpr_ready = sem("wpr_ready")
        wfcT_filled = sem("wfcT_filled")
        wprT_filled = sem("wprT_filled")
        wT_copied = sem("wT_copied")
        stats_ready = sem("stats_ready")
        rstd_ready = sem("rstd_ready")
        xn_ready = sem("xn_ready")
        xT_filled = sem("xT_filled")
        xT_copied = sem("xT_copied")
        h_filled = sem("h_filled")
        relu_ready = sem("relu_ready")
        sq_ready = sem("sq_ready")
        y_filled = sem("y_filled")
        y_ready = sem("y_ready")
        stored = [sem("stored0"), sem("stored1")]

        def pe_program(pe):
            def turn(c):
                pe.wait_ge(xn_ready, c + 1)
                for t in range(NT):
                    last = pe.transpose(M[:, t * P:(t + 1) * P], xn[:, t, :], C["ident"][:, :])
                last.then_inc(xT_filled, 1)

            pe.wait_ge(w_loaded, 16 * 6)
            pe.matmul(M[0:R, 0:P], fbT[:, :], vv[:, :], start=True, stop=True).then_inc(fv_filled, 1)
            pe.wait_ge(fv_copied, 1)
            for k in range(KC):
                last = pe.matmul(HB[:, 0, k * P:(k + 1) * P], uT[:, k * P:(k + 1) * P], fv[:, :],
                                 start=(k == 0), stop=(k == KC - 1), skip_group_check=True)
            last.then_inc(low_filled, 1)
            pe.wait_ge(wfc_ready, 1)
            for k in range(KC):
                last = pe.transpose(HB[:, 1, k * P:(k + 1) * P], wfc[:, k, :], C["ident"][:, :])
            last.then_inc(wfcT_filled, 1)
            pe.wait_ge(wpr_ready, 1)
            for k in range(KC):
                last = pe.transpose(HB[:, 2, k * P:(k + 1) * P], wpr[:, k * P:(k + 1) * P],
                                    C["ident"][:, :])
            last.then_inc(wprT_filled, 1)
            pe.wait_ge(wT_copied, 2)

            def step(b, par, first, last_b):
                pe.wait_ge(xT_copied, b + 1)
                for k in range(KC):
                    if not first:
                        pe.wait_ge(relu_ready, KC * b + k - KC + 1)
                    pe.matmul(HB[:, k, :], wfcT[:, k, :], xT[:, :], start=True, stop=True
                              ).then_inc(h_filled, 1)
                if not last_b:
                    turn(b + 1)
                if b is not None and not (isinstance(b, int) and b < 2):
                    pe.wait_ge(y_ready, b - 1)
                pe.wait_ge(sq_ready, KC * b + KC)
                for t in range(NT):
                    for k in range(KC):
                        last = pe.matmul(Y[:, par, t * P:(t + 1) * P], r2[:, k, t * P:(t + 1) * P],
                                         wprT[:, k, :], start=(t == 0 and k == 0),
                                         stop=(k == KC - 1), skip_group_check=True)
                last.then_inc(y_filled, 1)

            turn(0)
            pairs_of_batches(pe, NB, step)

        def act_program(act):
            act.wait_ge(fv_filled, 1)
            act.activation(fv[:, :], M[0:R, 0:P], ACT.Copy).then_inc(fv_copied, 1)
            act.wait_ge(wfcT_filled, 1)
            act.activation(wfcT[:, :, :], HB[:, 1, :].rearrange("p (k n) -> p k n", k=KC), ACT.Copy
                           ).then_inc(wT_copied, 1)
            act.wait_ge(wprT_filled, 1)
            act.activation(wprT[:, :, :], HB[:, 2, :].rearrange("p (k n) -> p k n", k=KC), ACT.Copy
                           ).then_inc(wT_copied, 1)

            def copy_xT(c):
                act.wait_ge(xT_filled, c + 1)
                act.activation(xT[:, :], M[:, :], ACT.Copy).then_inc(xT_copied, 1)

            def step(b, par, first, last_b):
                for k in range(KC):
                    act.wait_ge(h_filled, KC * b + k + 1)
                    if not first:
                        act.wait_ge(sq_ready, KC * b + k - KC + 1)
                    act.activation(r1[:, k, :], HB[:, k, :], ACT.Relu).then_inc(relu_ready, 1)
                if not last_b:
                    copy_xT(b + 1)

            copy_xT(0)
            pairs_of_batches(act, NB, step)

        def pool_program(pool):
            def rsqrt_stats(c):
                pool.wait_ge(stats_ready, c + 1)
                pool.tensor_tensor(rstd[:, :], mv[:, :, 1], C["ln_eps"][:, :], ALU.add)
                pool.drain()
                pool.tensor_tensor(rstd[:, :], rstd[:, :], C["half"][:, 0:NT], ALU.pow
                                   ).then_inc(rstd_ready, 1)

            def step(b, par, first, last_b):
                if not last_b:
                    rsqrt_stats(b + 1)

            rsqrt_stats(0)
            pairs_of_batches(pool, NB, step)

        def dve_program(v):
            def ternarise(w, rows, o):
                n = w.shape[-1]
                for i in range(rows):
                    wi = w[:, i, :] if rows > 1 else w
                    v.tensor_reduce(scl[:, o + i:o + i + 1], wi, AX.X, ALU.add,
                                    apply_absolute_value=True)
                v.drain()
                v.tensor_scalar(scl[:, o:o + rows], scl[:, o:o + rows], 1.0 / n, 1e-5, ALU.mult,
                                ALU.max)
                v.drain()
                v.reciprocal(rcp[:, o:o + rows], scl[:, o:o + rows])
                v.drain()
                for i in range(rows):
                    wi = w[:, i, :] if rows > 1 else w
                    ti = tern[:, i, :] if rows > 1 else tern[:, :, :].rearrange("p k n -> p (k n)")
                    v.tensor_scalar(ti, wi, rcp[:, o + i:o + i + 1], 2.0, ALU.mult, ALU.min)
                    v.drain()
                    v.tensor_scalar(ti, ti, -2.0, MAGIC, ALU.max, ALU.add)
                    v.drain()
                    v.tensor_scalar(ti, ti, MAGIC, 1.0, ALU.subtract, ALU.min)
                    v.drain()
                    v.tensor_scalar(ti, ti, -1.0, None, ALU.max)
                    v.drain()
                    v.tensor_tensor(ti, ti, wi, ALU.subtract)
                    v.drain()
                    v.tensor_tensor(ti, ti, wi, ALU.add)
                    v.drain()
                    last = v.tensor_scalar(wi, ti, scl[:, o + i:o + i + 1], None, ALU.mult)
                return last

            def normalise(c):
                for t in range(NT):
                    v.bn_stats(stats[:, t, :], tile_of(XT, c, t))
                v.drain()
                for t in range(NT):
                    last = v.bn_aggr(mv[:, t, :], stats[:, t, :])
                last.then_inc(stats_ready, 1)
                v.wait_ge(rstd_ready, c + 1)
                if not (isinstance(c, int) and c == 0):
                    v.wait_ge(xT_filled, c)
                for t in range(NT):
                    last = v.tensor_scalar(xn[:, t, :], tile_of(XT, c, t), mv[:, t, 0:1],
                                           rstd[:, t:t + 1], ALU.subtract, ALU.mult)
                last.then_inc(xn_ready, 1)

            v.wait_ge(w_loaded, 16 * 6)
            ternarise(wfc[:, :, :], KC, 0)
            v.drain()
            v.wait_ge(low_filled, 1)
            v.scalar_tensor_tensor(out=wfc[:, :, :].rearrange("p k n -> p (k n)"), in0=HB[:, 0, :],
                                   scalar=gate[:, 0:1],
                                   in1=wfc[:, :, :].rearrange("p k n -> p (k n)"), op0=ALU.mult,
                                   op1=ALU.add).then_inc(wfc_ready, 1)
            ternarise(wpr[:, :], 1, 4).then_inc(wpr_ready, 1)
            normalise(0)

            def step(b, par, first, last_b):
                for k in range(KC):
                    v.wait_ge(relu_ready, KC * b + k + 1)
                    if not first:
                        v.wait_ge(y_filled, b)
                    v.tensor_tensor(r2[:, k, :], r1[:, k, :], r1[:, k, :], ALU.mult
                                    ).then_inc(sq_ready, 1)
                if not last_b:
                    normalise(b + 1)
                v.wait_ge(y_filled, b + 1)
                if not (isinstance(b, int) and b < 2):
                    v.wait_ge(stored[par], 8 * b - 8 * par)
                v.tensor_tensor(yo[:, par, :, :], Y[:, par, :].rearrange("p (t n) -> p t n", t=NT),
                                XT[:, ds(4 * b, 4), :], ALU.add).then_inc(y_ready, 1)

            pairs_of_batches(v, NB, step)

        with nc.Block() as block:
            @block.sync
            def _(sp):
                sp.dma_start(wfc[:, :, :], C["wfc_dram"]).then_inc(w_loaded, 16)
                sp.dma_start(wpr[:, :], C["wpr_dram"]).then_inc(w_loaded, 16)
                sp.dma_start(uT[:, :], C["uT_dram"]).then_inc(w_loaded, 16)
                sp.dma_start(fbT[:, :], C["fbT_dram"]).then_inc(w_loaded, 16)
                sp.dma_start(vv[:, :], C["v_dram"]).then_inc(w_loaded, 16)
                sp.dma_start(gate[:, :], C["gate_dram"].to_broadcast([P, 1])).then_inc(w_loaded, 16)
                for b in range(NB):
                    sp.wait_ge(y_ready, b + 1)
                    sp.dma_start(C["out_dram"][b].rearrange("(t p) d -> p t d", p=P),
                                 yo[:, b % 2, :, :]).then_inc(stored[b % 2], 16)
                for par in range(2):
                    sp.wait_ge(stored[par], 16 * (NB // 2))

            block.tensor(pe_program)
            block.scalar(act_program)
            block.gpsimd(pool_program)
            block.vector(dve_program)


def to_channels(nc, C, XT, XC, NB):
    with ExitStack() as ctx:
        def sb(name, shape, dt=F32):
            return ctx.enter_context(nc.sbuf_tensor("tc_" + name, shape, dt))

        def sem(name):
            return C["sems"].enter_context(nc.semaphore("tc_" + name))

        stats = sb("stats", [P, NT, 6])
        mv = sb("mv", [P, 2, NT, 2])
        rstd = sb("rstd", [P, 2, NT])
        xn = sb("xn", [P, 2, NT, P])
        M = ctx.enter_context(nc.psum_tensor("tc_M", [P, 2, 512], F32))
        stats_ready = sem("stats_ready")
        rstd_ready = sem("rstd_ready")
        xn_ready = sem("xn_ready")
        x_turned = sem("x_turned")
        x_copied = sem("x_copied")

        def pe_program(pe):
            def step(b, par, first, last_b):
                pe.wait_ge(xn_ready, b + 1)
                if not (isinstance(b, int) and b < 2):
                    pe.wait_ge(x_copied, b - 1)
                for t in range(NT):
                    last = pe.transpose(M[:, par, t * P:(t + 1) * P], xn[:, par, t, :],
                                        C["ident"][:, :])
                last.then_inc(x_turned, 1)
            pairs_of_batches(pe, NB, step)

        def act_program(act):
            def step(b, par, first, last_b):
                act.wait_ge(x_turned, b + 1)
                act.activation(XC[:, ds(b, 1), :].rearrange("p a n -> p (a n)"), M[:, par, :],
                               ACT.Copy).then_inc(x_copied, 1)
            pairs_of_batches(act, NB, step)

        def pool_program(pool):
            def step(b, par, first, last_b):
                pool.wait_ge(stats_ready, b + 1)
                pool.tensor_tensor(rstd[:, par, :], mv[:, par, :, 1], C["ln_eps"][:, :], ALU.add)
                pool.drain()
                pool.tensor_tensor(rstd[:, par, :], rstd[:, par, :], C["half"][:, 0:NT], ALU.pow
                                   ).then_inc(rstd_ready, 1)
            pairs_of_batches(pool, NB, step)

        def dve_program(v):
            def measure(b, par):
                if not (isinstance(b, int) and b == 0):
                    v.wait_ge(stats_ready, b)
                for t in range(NT):
                    v.bn_stats(stats[:, t, :], tile_of(XT, b, t))
                v.drain()
                for t in range(NT):
                    last = v.bn_aggr(mv[:, par, t, :], stats[:, t, :])
                last.then_inc(stats_ready, 1)

            def step(b, par, first, last_b):
                if not last_b:
                    measure(b + 1, 1 - par)
                v.wait_ge(rstd_ready, b + 1)
                if not (isinstance(b, int) and b < 2):
                    v.wait_ge(x_turned, b - 1)
                for t in range(NT):
                    last = v.tensor_scalar(xn[:, par, t, :], tile_of(XT, b, t),
                                           mv[:, par, t, 0:1], rstd[:, par, t:t + 1],
                                           ALU.subtract, ALU.mult)
                last.then_inc(xn_ready, 1)
            measure(0, 0)
            pairs_of_batches(v, NB, step)

        with nc.Block() as block:
            block.tensor(pe_program)
            block.scalar(act_program)
            block.gpsimd(pool_program)
            block.vector(dve_program)


def from_channels(nc, C, XT, XC, NB):
    with ExitStack() as ctx:
        M = ctx.enter_context(nc.psum_tensor("fc_M", [P, 2, 512], F32))
        XS = ctx.enter_context(nc.sbuf_tensor("fc_XS", [P, 2, SEQ], F32))
        staged = C["sems"].enter_context(nc.semaphore("fc_staged"))
        back_turned = C["sems"].enter_context(nc.semaphore("fc_back_turned"))
        back_added = C["sems"].enter_context(nc.semaphore("fc_back_added"))

        def pe_program(pe):
            def step(b, par, first, last_b):
                if not (isinstance(b, int) and b < 2):
                    pe.wait_ge(back_added, b - 1)
                pe.wait_ge(staged, b + 1)
                for t in range(NT):
                    last = pe.transpose(M[:, par, t * P:(t + 1) * P],
                                        XS[:, par, t * P:(t + 1) * P], C["ident"][:, :])
                last.then_inc(back_turned, 1)
            pairs_of_batches(pe, NB, step)

        def act_program(act):
            def step(b, par, first, last_b):
                if not (isinstance(b, int) and b < 2):
                    act.wait_ge(back_turned, b - 1)
                act.activation(XS[:, par, :], XC[:, ds(b, 1), :].rearrange("p a n -> p (a n)"),
                               ACT.Copy).then_inc(staged, 1)
            pairs_of_batches(act, NB, step)

        def dve_program(v):
            def step(b, par, first, last_b):
                v.wait_ge(back_turned, b + 1)
                x = XT[:, ds(4 * b, 4), :]
                v.tensor_tensor(x, M[:, par, :].rearrange("p (t n) -> p t n", t=NT), x, ALU.add
                                ).then_inc(back_added, 1)
            pairs_of_batches(v, NB, step)

        with nc.Block() as block:
            block.tensor(pe_program)
            block.scalar(act_program)
            block.vector(dve_program)


BQ, BK, BV, BO, S1, B1, FB2, S2, B2, FB1, BQ1, BK1 = 0, 1, 2, 3, 4, 5, 6, 7, 8, 9, 13, 14
NPRM = 15


def linear_blocks(nc, C, XC, NBLK, NB):
    NG = NBLK * NB
    SHIFT = NB.bit_length() - 1
    KC = 4
    EPS = 1e-6

    with ExitStack() as ctx:
        def sb(name, shape, dt=F32):
            return ctx.enter_context(nc.sbuf_tensor("lb_" + name, shape, dt))

        def ps(name, shape, dt=F32):
            return ctx.enter_context(nc.psum_tensor("lb_" + name, shape, dt))

        def sem(name):
            return C["sems"].enter_context(nc.semaphore("lb_" + name))

        prm = sb("prm", [P, NPRM, NBLK + 1])
        wqkv = sb("wqkv", [P, 3, P])
        wo = sb("wo", [P, P])
        w1 = sb("w1", [P, KC, P])
        w2 = sb("w2", [P, KC, P])
        eps = sb("eps", [P, 1])
        eq = sb("eq", [P, SEQ])
        ek = sb("ek", [P, SEQ])
        fq = sb("fq", [P, SEQ])
        fk = sb("fk", [P, SEQ])
        kv = sb("kv", [P, SEQ])
        ksum = sb("ksum", [P, 1])
        kvsum = sb("kvsum", [P, 1])
        lt = sb("lt", [P, SEQ])
        rt = sb("rt", [P, SEQ])
        att = sb("att", [P, SEQ])
        ao = sb("ao", [P, SEQ])
        y1 = sb("y1", [P, SEQ])
        z1 = sb("z1", [P, NT, P])
        x1 = sb("x1", [P, 2, SEQ])
        h = sb("h", [P, KC, SEQ])
        ff = sb("ff", [P, SEQ])
        y2 = sb("y2", [P, SEQ])
        z2 = sb("z2", [P, NT, P])
        stats1 = sb("stats1", [P, NT, 6])
        stats2 = sb("stats2", [P, NT, 6])
        mv1 = sb("mv1", [P, NT, 2])
        mv2 = sb("mv2", [P, NT, 2])
        rstd1 = sb("rstd1", [P, NT])
        rstd2 = sb("rstd2", [P, NT])

        Q = ps("Q", [P, 512])
        K = ps("K", [P, 512])
        V = ps("V", [P, 512])
        H = ps("H", [P, 2, 512])
        FF = ps("FF", [P, 512])
        M1 = ps("M1", [P, 512])
        M2 = ps("M2", [P, 512])

        prm_loaded = sem("prm_loaded")
        prm_ready = sem("prm_ready")
        wqkv_loaded = sem("wqkv_loaded")
        wo_loaded = sem("wo_loaded")
        w1_loaded = sem("w1_loaded")
        w2_loaded = sem("w2_loaded")
        q_filled = sem("q_filled")
        k_filled = sem("k_filled")
        v_filled = sem("v_filled")
        eq_ready = sem("eq_ready")
        ek_ready = sem("ek_ready")
        fq_ready = sem("fq_ready")
        fk_ready = sem("fk_ready")
        kv_ready = sem("kv_ready")
        rt_ready = sem("rt_ready")
        att_ready = sem("att_ready")
        o_filled = sem("o_filled")
        ao_ready = sem("ao_ready")
        y1_ready = sem("y1_ready")
        y1_turned = sem("y1_turned")
        stats1_ready = sem("stats1_ready")
        rstd1_ready = sem("rstd1_ready")
        z1_ready = sem("z1_ready")
        z1_turned = sem("z1_turned")
        x1_ready = sem("x1_ready")
        h_filled = sem("h_filled")
        h_ready = sem("h_ready")
        ff_filled = sem("ff_filled")
        ff_ready = sem("ff_ready")
        y2_ready = sem("y2_ready")
        y2_turned = sem("y2_turned")
        stats2_ready = sem("stats2_ready")
        rstd2_ready = sem("rstd2_ready")
        z2_ready = sem("z2_ready")
        z2_turned = sem("z2_turned")
        x_ready = sem("x_ready")

        def block_of(i):
            return i // NB if isinstance(i, int) else i >> SHIFT

        def state(i):
            b = i % NB if isinstance(i, int) else i & (NB - 1)
            return XC[:, ds(b, 1), :].rearrange("p a n -> p (a n)")

        def x1_of(i):
            return x1[:, ds(i % 2 if isinstance(i, int) else i & 1, 1), :].rearrange(
                "p a n -> p (a n)")

        def col(kind, i):
            return prm[:, kind, ds(block_of(i), 1)]

        def steps(eng, part):
            def fixed(g):
                part(g, g >= NB, lambda k: 0 <= g - k < NG)
            for g in range(4):
                fixed(g)
            with eng.Fori(4, NB) as g:
                part(g, False, lambda k: True)
            with eng.Fori(NB, NG) as g:
                part(g, True, lambda k: True)
            for g in range(NG, NG + 4):
                fixed(g)

        def reused(i):
            return not (isinstance(i, int) and i == 0)

        def pe_program(pe):
            def project_q(g, old):
                pe.wait_ge(wqkv_loaded, 16 * block_of(g) + 16)
                if old:
                    pe.wait_ge(x_ready, g - NB + 1)
                if reused(g):
                    pe.wait_ge(fq_ready, g)
                pe.matmul(Q[:, :], wqkv[:, 0, :], state(g), start=True, stop=True
                          ).then_inc(q_filled, 1)

            def project_k(g):
                if reused(g):
                    pe.wait_ge(fk_ready, g)
                pe.matmul(K[:, :], wqkv[:, 1, :], state(g), start=True, stop=True
                          ).then_inc(k_filled, 1)

            def project_v(g):
                if reused(g):
                    pe.wait_ge(kv_ready, g)
                pe.matmul(V[:, :], wqkv[:, 2, :], state(g), start=True, stop=True
                          ).then_inc(v_filled, 1)

            def turn_y2(i):
                pe.wait_ge(y2_ready, i + 1)
                if reused(i):
                    pe.wait_ge(x_ready, i)
                for t in range(NT):
                    last = pe.transpose(M2[:, t * P:(t + 1) * P], y2[:, t * P:(t + 1) * P],
                                        C["ident"][:, :])
                last.then_inc(y2_turned, 1)

            def turn_z1(i):
                pe.wait_ge(z1_ready, i + 1)
                for t in range(NT):
                    last = pe.transpose(M1[:, t * P:(t + 1) * P], z1[:, t, :], C["ident"][:, :])
                last.then_inc(z1_turned, 1)

            def attention_out(i):
                pe.wait_ge(wo_loaded, 16 * block_of(i) + 16)
                if not (isinstance(i, int) and i < 2):
                    pe.wait_ge(ff_ready, i - 1)
                elif i == 1:
                    pe.wait_ge(ao_ready, 1)
                pe.wait_ge(att_ready, i + 1)
                pe.matmul(FF[:, :], wo[:, :], att[:, :], start=True, stop=True
                          ).then_inc(o_filled, 1)

            def turn_y1(i):
                pe.wait_ge(y1_ready, i + 1)
                if reused(i):
                    pe.wait_ge(x1_ready, i)
                for t in range(NT):
                    last = pe.transpose(M1[:, t * P:(t + 1) * P], y1[:, t * P:(t + 1) * P],
                                        C["ident"][:, :])
                last.then_inc(y1_turned, 1)

            def turn_z2(i):
                pe.wait_ge(z2_ready, i + 1)
                for t in range(NT):
                    last = pe.transpose(M2[:, t * P:(t + 1) * P], z2[:, t, :], C["ident"][:, :])
                last.then_inc(z2_turned, 1)

            def up(i, k):
                if k == 0:
                    pe.wait_ge(w1_loaded, 16 * block_of(i) + 16)
                    pe.wait_ge(x1_ready, i + 1)
                    if reused(i):
                        pe.wait_ge(h_ready, KC * i)
                if k >= 2:
                    pe.wait_ge(h_ready, KC * i + k - 1)
                pe.matmul(H[:, k % 2, :], w1[:, k, :], x1_of(i), start=True, stop=True
                          ).then_inc(h_filled, 1)

            def down(i, k, projected):
                if k == 0:
                    pe.wait_ge(w2_loaded, 16 * block_of(i) + 16)
                    if projected:
                        pe.wait_ge(ao_ready, i + 2)
                    elif reused(i):
                        pe.wait_ge(ff_ready, i)
                pe.wait_ge(h_ready, KC * i + k + 1)
                pe.matmul(FF[:, :], w2[:, k, :], h[:, k, :], start=(k == 0),
                          stop=(k == KC - 1)).then_inc(ff_filled, 1)

            def part(g, old, on):
                if on(0):
                    project_q(g, old)
                if on(2):
                    turn_z1(g - 2)
                if on(0):
                    project_k(g)
                if on(4):
                    turn_z2(g - 4)
                if on(0):
                    project_v(g)
                if on(2):
                    up(g - 2, 0)
                if on(1):
                    attention_out(g - 1)
                if on(2):
                    up(g - 2, 1)
                if on(3):
                    turn_y2(g - 3)
                if on(2):
                    down(g - 2, 0, on(1))
                    up(g - 2, 2)
                if on(1):
                    turn_y1(g - 1)
                if on(2):
                    down(g - 2, 1, on(1))
                    up(g - 2, 3)
                    down(g - 2, 2, on(1))
                    down(g - 2, 3, on(1))

            steps(pe, part)

        def act_program(act):
            def part(g, old, on):
                if on(1):
                    i = g - 1
                    act.preload_act_table_set("natural_log_exp_and_others")
                    act.wait_ge(fq_ready, i + 1)
                    act.wait_ge(fk_ready, i + 1)
                    act.activation(lt[:, :], fq[:, :], ACT.Ln, scale=ksum[:, 0:1],
                                   bias=eps[:, 0:1])
                    act.drain()
                    if reused(i):
                        act.wait_ge(att_ready, i)
                    act.activation(rt[:, :], lt[:, :], ACT.Exp, scale=-1.0).then_inc(rt_ready, 1)
                elif on(0):
                    act.preload_act_table_set("natural_log_exp_and_others")
                    act.wait_ge(prm_ready, 1)
                if on(0):
                    act.wait_ge(q_filled, g + 1)
                    if reused(g):
                        act.wait_ge(fq_ready, g)
                    act.activation(eq[:, :], Q[:, :], ACT.Exp, bias=col(BQ, g)
                                   ).then_inc(eq_ready, 1)
                    act.wait_ge(k_filled, g + 1)
                    if reused(g):
                        act.wait_ge(fk_ready, g)
                    act.activation(ek[:, :], K[:, :], ACT.Exp, bias=col(BK, g)
                                   ).then_inc(ek_ready, 1)
                if on(1) or on(2):
                    act.preload_act_table_set("gelu_apprx_tanh_and_others")
                if on(1):
                    i = g - 1
                    act.wait_ge(o_filled, i + 1)
                    if reused(i):
                        act.wait_ge(y1_ready, i)
                    act.activation(ao[:, :], FF[:, :], ACT.Gelu_apprx_tanh, bias=col(BO, i)
                                   ).then_inc(ao_ready, 1)
                if on(2):
                    i = g - 2
                    for k in range(KC):
                        act.wait_ge(h_filled, KC * i + k + 1)
                        if reused(i):
                            act.wait_ge(ff_filled, KC * i - KC + k + 1)
                        act.activation(h[:, k, :], H[:, k % 2, :], ACT.Gelu_apprx_tanh,
                                       bias=col(FB1 + k, i)).then_inc(h_ready, 1)
                    act.wait_ge(ff_filled, KC * i + KC)
                    if reused(i):
                        act.wait_ge(y2_ready, i)
                    act.activation(ff[:, :], FF[:, :], ACT.Gelu_apprx_tanh, bias=col(FB2, i)
                                   ).then_inc(ff_ready, 1)

            steps(act, part)

        def pool_program(pool):
            def rsqrt_stats(i, ready, mv, out, done):
                pool.wait_ge(ready, i + 1)
                pool.tensor_tensor(out[:, :], mv[:, :, 1], eps[:, 0:1].to_broadcast([P, NT]), ALU.add)
                pool.drain()
                pool.tensor_tensor(out[:, :], out[:, :], C["half"][:, 0:NT], ALU.pow
                                   ).then_inc(done, 1)

            def part(g, old, on):
                if on(3):
                    i = g - 3
                    pool.wait_ge(ff_ready, i + 1)
                    if reused(i):
                        pool.wait_ge(y2_turned, i)
                    pool.tensor_tensor(y2[:, :], ff[:, :], x1_of(i), ALU.add).then_inc(y2_ready, 1)
                if on(1):
                    rsqrt_stats(g - 1, stats1_ready, mv1, rstd1, rstd1_ready)
                if on(3):
                    rsqrt_stats(g - 3, stats2_ready, mv2, rstd2, rstd2_ready)

            steps(pool, part)

        def dve_program(v):
            def measure(M, stats, mv, ready):
                for t in range(NT):
                    v.bn_stats(stats[:, t, :], M[:, t * P:(t + 1) * P])
                v.drain()
                for t in range(NT):
                    last = v.bn_aggr(mv[:, t, :], stats[:, t, :])
                last.then_inc(ready, 1)

            def centre(M, mv, rstd, z, ready):
                for t in range(NT):
                    last = v.tensor_scalar(z[:, t, :], M[:, t * P:(t + 1) * P], mv[:, t, 0:1],
                                           rstd[:, t:t + 1], ALU.subtract, ALU.mult)
                last.then_inc(ready, 1)

            def elu_plus_1(e):
                v.tensor_scalar(e[:, :], e[:, :], 1.0, -1.0, ALU.min, ALU.add)
                v.drain()
                v.tensor_scalar(e[:, :], e[:, :], 1.0, None, ALU.add)
                v.drain()

            def part(g, old, on):
                if on(4):
                    i = g - 4
                    v.wait_ge(rstd2_ready, i + 1)
                    if reused(i):
                        v.wait_ge(z2_turned, i)
                    centre(M2, mv2, rstd2, z2, z2_ready)
                if on(2):
                    i = g - 2
                    v.wait_ge(z1_turned, i + 1)
                    if not (isinstance(i, int) and i < 2):
                        v.wait_ge(y2_ready, i - 1)
                        v.wait_ge(h_filled, KC * i - KC)
                    v.tensor_scalar(x1_of(i), M1[:, :], col(S1, i), col(B1, i), ALU.mult, ALU.add
                                    ).then_inc(x1_ready, 1)
                if on(4):
                    i = g - 4
                    v.wait_ge(z2_turned, i + 1)
                    v.tensor_scalar(state(i), M2[:, :], col(S2, i), col(B2, i), ALU.mult, ALU.add
                                    ).then_inc(x_ready, 1)
                if on(1):
                    i = g - 1
                    v.wait_ge(rt_ready, i + 1)
                    v.wait_ge(kv_ready, i + 1)
                    if reused(i):
                        v.wait_ge(o_filled, i)
                    v.scalar_tensor_tensor(out=att[:, :], in0=fq[:, :], scalar=kvsum[:, 0:1],
                                           in1=rt[:, :], op0=ALU.mult, op1=ALU.mult
                                           ).then_inc(att_ready, 1)
                if on(0):
                    v.wait_ge(eq_ready, g + 1)
                    elu_plus_1(eq)
                    v.scalar_tensor_tensor(out=fq[:, :], in0=Q[:, :], scalar=col(BQ1, g),
                                           in1=eq[:, :], op0=ALU.add, op1=ALU.max
                                           ).then_inc(fq_ready, 1)
                    v.wait_ge(ek_ready, g + 1)
                    elu_plus_1(ek)
                if on(1):
                    i = g - 1
                    v.wait_ge(ao_ready, i + 1)
                    if reused(i):
                        v.wait_ge(y1_turned, i)
                    v.tensor_tensor(y1[:, :], ao[:, :], state(i), ALU.add).then_inc(y1_ready, 1)
                if on(0):
                    v.scalar_tensor_tensor(out=fk[:, :], in0=K[:, :], scalar=col(BK1, g),
                                           in1=ek[:, :], op0=ALU.add, op1=ALU.max,
                                           accum_out=ksum[:, 0:1]).then_inc(fk_ready, 1)
                    v.wait_ge(v_filled, g + 1)
                    v.wait_ge(fk_ready, g + 1)
                    v.scalar_tensor_tensor(out=kv[:, :], in0=V[:, :], scalar=col(BV, g),
                                           in1=fk[:, :], op0=ALU.add, op1=ALU.mult,
                                           accum_out=kvsum[:, 0:1]).then_inc(kv_ready, 1)
                if on(1):
                    v.wait_ge(y1_turned, g - 1 + 1)
                    measure(M1, stats1, mv1, stats1_ready)
                if on(3):
                    v.wait_ge(y2_turned, g - 3 + 1)
                    measure(M2, stats2, mv2, stats2_ready)
                if on(1):
                    i = g - 1
                    v.wait_ge(rstd1_ready, i + 1)
                    if reused(i):
                        v.wait_ge(z1_turned, i)
                    centre(M1, mv1, rstd1, z1, z1_ready)

            v.memset(eps[:, :], EPS)
            v.drain()
            v.wait_ge(prm_loaded, 16)
            v.tensor_scalar(prm[:, BQ1:BK1 + 1, 0:NBLK], prm[:, BQ:BK + 1, 0:NBLK], 1.0, None, ALU.add
                            ).then_inc(prm_ready, 1)
            v.drain()
            steps(v, part)

        with nc.Block() as block:
            @block.sync
            def _(sp):
                sp.dma_start(prm[:, 0:BQ1, 0:NBLK], C["prm_dram"]).then_inc(prm_loaded, 16)

                def load(k, used):
                    if used:
                        sp.wait_ge(v_filled, NB * k)
                    sp.dma_start(wqkv[:, :, :], C["bqkv_dram"][k].rearrange(
                        "p (c n) -> p c n", c=3)).then_inc(wqkv_loaded, 16)
                    if used:
                        sp.wait_ge(o_filled, NB * k)
                    sp.dma_start(wo[:, :], C["bwo_dram"][k]).then_inc(wo_loaded, 16)
                    if used:
                        sp.wait_ge(h_filled, KC * NB * k)
                    sp.dma_start(w1[:, :, :], C["bw1_dram"][k].rearrange(
                        "p (c n) -> p c n", c=KC)).then_inc(w1_loaded, 16)
                    if used:
                        sp.wait_ge(ff_filled, KC * NB * k)
                    sp.dma_start(w2[:, :, :], C["bw2_dram"][k].rearrange(
                        "(c p) n -> p c n", p=P)).then_inc(w2_loaded, 16)

                load(0, False)
                for k in range(1, NBLK):
                    load(k, True)

            block.tensor(pe_program)
            block.scalar(act_program)
            block.gpsimd(pool_program)
            block.vector(dve_program)


def layer_stack_kernel(nc, C):
    NB, NBLK = C["x_dram"].shape[0], C["bqkv_dram"].shape[0]
    NTILES = NB * NT
    with ExitStack() as sems, ExitStack() as ctx:
        def sb(name, shape, dt=F32):
            return ctx.enter_context(nc.sbuf_tensor(name, shape, dt))

        C = dict(C, sems=sems)
        XT = sb("XT", [P, NTILES, P])
        ident = sb("ident", [P, P])
        identb = sb("identb", [P, P], BF16)
        half = sb("half", [P, NT])
        rms_eps = sb("rms_eps", [P, 1])
        ln_eps = sb("ln_eps", [P, NT])
        iota8 = sb("iota8", [P, 8])
        C = dict(C, ident=ident, identb=identb, half=half, ln_eps=ln_eps, rms_eps=rms_eps, iota8=iota8)
        const_loaded = ctx.enter_context(nc.semaphore("const_loaded"))
        masks_loaded = ctx.enter_context(nc.semaphore("masks_loaded"))

        with nc.sbuf_tensor("H", [P, NTILES, P], F32) as H:
            with ExitStack() as actx:
                cos = actx.enter_context(nc.sbuf_tensor("cos", [P, NT, HD], F32))
                masks = actx.enter_context(nc.sbuf_tensor("masks", [P, 2, P], F32))
                maskT = actx.enter_context(nc.sbuf_tensor("maskT", [P, 512], BF16))
                maskQ = actx.enter_context(nc.sbuf_tensor("maskQ", [P, 512], BF16))
                sins = actx.enter_context(nc.sbuf_tensor("sins", [P, 2, NT, HD], F32))
                with nc.Block() as block:
                    @block.sync
                    def _(sp):
                        sp.dma_start(ident[:, :], C["ident_dram"]).then_inc(const_loaded, 16)
                        sp.dma_start(iota8[:, :], C["iota8_dram"]).then_inc(const_loaded, 16)
                        sp.dma_start(cos[:, :, :], C["cos_dram"]).then_inc(const_loaded, 16)
                        sp.dma_start(sins[:, :, :, :], C["sin_dram"]).then_inc(const_loaded, 16)
                        sp.dma_start(masks[:, :, :], C["masks_dram"]).then_inc(const_loaded, 16)
                        sp.wait_ge(const_loaded, 80)

                    @block.vector
                    def _(v):
                        v.memset(half[:, :], -0.5)
                        v.memset(ln_eps[:, :], LN_EPS)
                        v.memset(rms_eps[:, :], 2.0 ** -23)
                        v.wait_ge(const_loaded, 80)
                        v.tensor_copy(identb[:, :], ident[:, :])
                        for i, m in enumerate((maskT, maskQ)):
                            v.tensor_copy(m[:, :].rearrange("p (a n) -> p a n", a=NT),
                                          masks[:, i:i + 1, :].to_broadcast([P, NT, P]))
                A = dict(C, cos=cos, maskT=maskT, maskQ=maskQ)
                attention_stage(nc, dict(A, sin=sins[:, 0, :, :], wqkv_dram=C["a_wqkv_dram"],
                                         wout_dram=C["a_wout_dram"], stage_loads=96),
                                XT, XT, "da_", False, NB)
                attention_stage(nc, dict(A, sin=sins[:, 1, :, :], wqkv_dram=C["g_wqkv_dram"],
                                         wout_dram=C["g_wout_dram"], stage_loads=48),
                                XT, H, "ga_", True, NB)
            expert_stage(nc, C, XT, H, NB)
        with nc.sbuf_tensor("XC", [P, NB, SEQ], F32) as XC:
            to_channels(nc, C, XT, XC, NB)
            linear_blocks(nc, C, XC, NBLK, NB)
            from_channels(nc, C, XT, XC, NB)
        ternary_stage(nc, C, XT, NB)


def kernel(**inputs):
    import numpy as np
    import concourse.bacc as bacc
    from concourse.bass_utils import run_bass_kernel_spmd

    i = {k: np.ascontiguousarray(v) for k, v in inputs.items()}
    B, T, D = i["L0_attn_x"].shape
    f = np.float32

    inv = (1.0 / f(10000.0) ** (np.arange(0, HD, 2, dtype=f) / f(HD))).astype(f)
    ang = np.outer(np.arange(T, dtype=f), inv).astype(f)
    c, s = np.cos(ang).astype(f), np.sin(ang).astype(f)
    cos = np.concatenate([c, c], 1).reshape(NT, P, HD).transpose(1, 0, 2)
    sins = np.stack([np.concatenate([s, -s], 1), np.concatenate([-s, s], 1)])
    sins = sins.reshape(2, NT, P, HD).transpose(2, 0, 1, 3)
    later = np.where(np.arange(P)[:, None] > np.arange(P)[None, :], f(BIG), f(0))
    masks = np.stack([later, later.T], 1)

    def columns(name, n):
        a = i["L1_attn_" + name]
        return a.reshape(a.shape[0], n, P).transpose(2, 1, 0)

    prm = np.concatenate([columns(n, 1) for n in
                          ("bq", "bk", "bv", "bo", "ln1_s", "ln1_b", "b2", "ln2_s", "ln2_b")]
                         + [columns("b1", 4)], 1)
    arrays = {
        "x": i["L0_attn_x"],
        "ident": np.eye(P, dtype=f),
        "iota8": np.tile(np.arange(8, dtype=f), (P, 1)),
        "cos": cos, "sin": sins, "masks": masks,
        "lam": np.stack([i["L0_attn_lambda_" + n] for n in ("q1", "k1", "q2", "k2")]),
        "a_wqkv": np.concatenate([i["L0_attn_" + n].T for n in ("Wq", "Wk", "Wv")], 1),
        "a_wout": i["L0_attn_Wproj"].T,
        "g_wqkv": np.concatenate([i["L0_ffn_" + n] for n in ("Wq", "Wk", "Wv")], 1),
        "g_wout": i["L0_ffn_Wo"],
        "ln1w": i["L0_ffn_ln1_w"].reshape(P, 1),
        "ln2w": i["L0_ffn_ln2_w"].reshape(P, 1),
        "wg": i["L0_ffn_Wg"].transpose(1, 0, 2),
        "wu": i["L0_ffn_Wu"].transpose(1, 0, 2),
        "wd": i["L0_ffn_Wd"].reshape(8, 2, P, P).transpose(2, 0, 1, 3),
        "wr": i["L0_ffn_Wr"],
        "prm": prm,
        "bqkv": np.concatenate([i["L1_attn_" + n] for n in ("Wq", "Wk", "Wv")], 2),
        "bwo": i["L1_attn_Wo"],
        "bw1": i["L1_attn_W1"],
        "bw2": i["L1_attn_W2"],
        "wfc": i["L1_ffn_w_fc"].reshape(4, P, P).transpose(1, 0, 2),
        "wpr": i["L1_ffn_w_proj"],
        "uT": i["L1_ffn_u"].T,
        "fbT": i["L1_ffn_fast_b"].T,
        "v": i["L1_ffn_v"],
        "gate": i["L1_ffn_gate"].reshape(1, 1),
    }
    nc = bacc.Bacc("TRN2", target_bir_lowering=False, num_devices=1)
    C, feed = {"lambda_init": 0.8 - 0.6 * float(np.exp(-0.3))}, {}
    for name, a in arrays.items():
        a = np.ascontiguousarray(a)
        feed[name + "_dram"] = a
        C[name + "_dram"] = nc.dram_tensor(name + "_dram", a.shape, F32,
                                           kind="ExternalInput").ap()
    C["out_dram"] = nc.dram_tensor("out_dram", (B, T, D), F32, kind="ExternalOutput").ap()
    layer_stack_kernel(nc, C)
    r = run_bass_kernel_spmd(nc, [feed], core_ids=[0])
    return r.results[0]["out_dram"]
```
